# Optimizing a Trainium2 kernel written in Bass

```python
import numpy as np
import jax
import jax.numpy as jnp

def _softmax(x, axis=-1):
    return jax.nn.softmax(x, axis=axis)

def _gelu(x):
    return jax.nn.gelu(x, approximate=True)

def _silu(x):
    return jax.nn.silu(x)

def _sigmoid(x):
    return jax.nn.sigmoid(x)

def _layernorm(x, axis=-1, eps=1e-05):
    m = jnp.mean(x, axis=axis, keepdims=True)
    v = jnp.var(x, axis=axis, keepdims=True)
    return (x - m) / jnp.sqrt(v + eps)

def _scatter_add(tgt, idx, src, axis=0):
    return tgt.at[idx].add(src)

def _segment_sum(src, seg, n):
    return jax.ops.segment_sum(src, seg, n)
kernel_name = 'mk_prb_d2_jaxref_r4_c51c51'

def setup_inputs(seed: int=0):
    np.random.seed(seed)
    _w = jnp.asarray

    def _L0_attn_setup():
        import jax, jax.numpy as jnp
        import numpy as np
        N_HEADS = 16
        EPS = 1e-06

        def _feature_map(x):
            return jax.nn.elu(x) + 1.0
        key = jax.random.key(seed)
        k1, k2, k3 = jax.random.split(key, 3)
        B, S, D = (1, 512, 256)
        x = jax.random.normal(k1, (B, S, D), dtype=jnp.float32)
        causal_mask = jnp.tril(jnp.ones((S, S), dtype=bool))[None, None]
        W_qkv = jax.random.normal(k2, (D, 3 * D), dtype=jnp.float32) / np.sqrt(D)
        W_out = jax.random.normal(k3, (D, D), dtype=jnp.float32) / np.sqrt(D)
        return {'x': x, 'causal_mask': causal_mask, 'W_qkv': W_qkv, 'W_out': W_out}
    _L0_attn_in = _L0_attn_setup()

    def _L0_ffn_setup():
        import jax, jax.numpy as jnp
        import numpy as np
        THRESH_FACTOR = 0.7

        def ternary_quantize(w):
            delta = THRESH_FACTOR * jnp.mean(jnp.abs(w))
            return jnp.where(w > delta, 1.0, jnp.where(w < -delta, -1.0, 0.0)).astype(w.dtype)
        key = jax.random.key(seed)
        k1, k2, k3 = jax.random.split(key, 3)
        B, S, D_IN, D_OUT = (8, 1024, 256, 256)
        inp = {'input': jax.random.normal(k1, (B, S, D_IN), dtype=jnp.float32), 'weight': jax.random.normal(k2, (D_OUT, D_IN), dtype=jnp.float32) * (1.0 / np.sqrt(D_IN)), 'alpha': jnp.ones((1,), dtype=jnp.float32), 'bias': jax.random.normal(k3, (D_OUT,), dtype=jnp.float32) * (1.0 / np.sqrt(D_IN))}
        return inp
    _L0_ffn_in = _L0_ffn_setup()

    def _L1_attn_setup():
        import jax, jax.numpy as jnp
        import numpy as np
        HIDDEN = 256
        NUM_HEADS = 16
        NUM_KV = 4
        HEAD_DIM = HIDDEN // NUM_HEADS
        GROUPS = NUM_HEADS // NUM_KV
        SCALE = HEAD_DIM ** 0.5
        key = jax.random.key(seed)
        ks = jax.random.split(key, 9)
        s = 0.02
        B, N = (4, 512)
        return {'x': jax.random.normal(ks[0], (B, N, HIDDEN), dtype=jnp.float32), 'Wq': jax.random.normal(ks[1], (HIDDEN, NUM_HEADS * HEAD_DIM), dtype=jnp.float32) * s, 'bq': jnp.zeros((NUM_HEADS * HEAD_DIM,), dtype=jnp.float32), 'Wk': jax.random.normal(ks[2], (HIDDEN, NUM_KV * HEAD_DIM), dtype=jnp.float32) * s, 'bk': jnp.zeros((NUM_KV * HEAD_DIM,), dtype=jnp.float32), 'Wv': jax.random.normal(ks[3], (HIDDEN, NUM_KV * HEAD_DIM), dtype=jnp.float32) * s, 'bv': jnp.zeros((NUM_KV * HEAD_DIM,), dtype=jnp.float32), 'Wo': jax.random.normal(ks[4], (NUM_HEADS * HEAD_DIM, HIDDEN), dtype=jnp.float32) * s, 'bo': jnp.zeros((HIDDEN,), dtype=jnp.float32)}
    _L1_attn_in = _L1_attn_setup()

    def _L1_ffn_setup():
        import jax, jax.numpy as jnp
        import numpy as np
        B, N, D, E, R, K = (4, 512, 256, 8, 64, 2)
        key = jax.random.key(seed)
        ks = jax.random.split(key, 5)
        scale = 0.02
        return {'x': jax.random.normal(ks[0], (B, N, D), dtype=jnp.float32), 'gate_w': jax.random.normal(ks[1], (D, E), dtype=jnp.float32) * scale, 'Wu': jax.random.normal(ks[2], (E, D, R), dtype=jnp.float32) * scale, 'Wv': jax.random.normal(ks[3], (E, D, R), dtype=jnp.float32) * scale, 'Wo': jax.random.normal(ks[4], (E, R, D), dtype=jnp.float32) * scale}
    _L1_ffn_in = _L1_ffn_setup()
    _d = {'L0_attn_x': _L0_attn_in['x'], 'L0_attn_causal_mask': _L0_attn_in['causal_mask'], 'L0_attn_W_qkv': _L0_attn_in['W_qkv'], 'L0_attn_W_out': _L0_attn_in['W_out'], 'L0_ffn_weight': _L0_ffn_in['weight'], 'L0_ffn_alpha': _L0_ffn_in['alpha'], 'L0_ffn_bias': _L0_ffn_in['bias'], 'L1_attn_Wq': _L1_attn_in['Wq'], 'L1_attn_bq': _L1_attn_in['bq'], 'L1_attn_Wk': _L1_attn_in['Wk'], 'L1_attn_bk': _L1_attn_in['bk'], 'L1_attn_Wv': _L1_attn_in['Wv'], 'L1_attn_bv': _L1_attn_in['bv'], 'L1_attn_Wo': _L1_attn_in['Wo'], 'L1_attn_bo': _L1_attn_in['bo'], 'L1_ffn_gate_w': _L1_ffn_in['gate_w'], 'L1_ffn_Wu': _L1_ffn_in['Wu'], 'L1_ffn_Wv': _L1_ffn_in['Wv'], 'L1_ffn_Wo': _L1_ffn_in['Wo']}
    _x0 = _d['L0_attn_x']
    _d['L0_attn_x'] = jax.random.normal(jax.random.fold_in(jax.random.key(seed), 1), (4, 2048, 256), dtype=_x0.dtype)
    del _x0
    return _d

def reference(L0_attn_x, L0_attn_causal_mask, L0_attn_W_qkv, L0_attn_W_out, L0_ffn_weight, L0_ffn_alpha, L0_ffn_bias, L1_attn_Wq, L1_attn_bq, L1_attn_Wk, L1_attn_bk, L1_attn_Wv, L1_attn_bv, L1_attn_Wo, L1_attn_bo, L1_ffn_gate_w, L1_ffn_Wu, L1_ffn_Wv, L1_ffn_Wo):

    def _L0_attn_ref(x, causal_mask, W_qkv, W_out):
        import jax, jax.numpy as jnp
        import numpy as np
        N_HEADS = 16
        EPS = 1e-06

        def _feature_map(x):
            return jax.nn.elu(x) + 1.0
        B, S, D = x.shape
        H = N_HEADS
        hd = D // H
        qkv = x @ W_qkv
        q, k, v = jnp.split(qkv, 3, axis=-1)

        def to_heads(t):
            return t.reshape(B, S, H, hd).transpose(0, 2, 1, 3)
        q, k, v = (to_heads(q), to_heads(k), to_heads(v))
        phi_q = _feature_map(q)
        phi_k = _feature_map(k)
        k_cum = jnp.cumsum(phi_k, axis=2)
        kv = jnp.einsum('bhsi,bhsj->bhsij', phi_k, v)
        kv_cum = jnp.cumsum(kv, axis=2)
        numer = jnp.einsum('bhsi,bhsij->bhsj', phi_q, kv_cum)
        denom = jnp.einsum('bhsi,bhsi->bhs', phi_q, k_cum) + EPS
        attn_out = numer / denom[..., None]
        attn_out = attn_out.transpose(0, 2, 1, 3).reshape(B, S, D)
        return attn_out @ W_out

    def _L0_ffn_ref(input, weight, alpha, bias):
        import jax, jax.numpy as jnp
        import numpy as np
        THRESH_FACTOR = 0.7

        def ternary_quantize(w):
            delta = THRESH_FACTOR * jnp.mean(jnp.abs(w))
            return jnp.where(w > delta, 1.0, jnp.where(w < -delta, -1.0, 0.0)).astype(w.dtype)
        w_ternary = ternary_quantize(weight)
        w_eff = w_ternary * alpha
        out = jnp.einsum('bsd,od->bso', input, w_eff) + bias
        return out

    def _L1_attn_ref(x, Wq, bq, Wk, bk, Wv, bv, Wo, bo):
        import jax, jax.numpy as jnp
        import numpy as np
        HIDDEN = 256
        NUM_HEADS = 16
        NUM_KV = 4
        HEAD_DIM = HIDDEN // NUM_HEADS
        GROUPS = NUM_HEADS // NUM_KV
        SCALE = HEAD_DIM ** 0.5
        B, N, _ = x.shape
        q = x @ Wq + bq
        k = x @ Wk + bk
        v = x @ Wv + bv
        q = q.reshape(B, N, NUM_HEADS, HEAD_DIM).transpose(0, 2, 1, 3)
        q = q.reshape(B, NUM_KV, GROUPS, N, HEAD_DIM).transpose(0, 2, 1, 3, 4)
        k = k.reshape(B, N, NUM_KV, HEAD_DIM).transpose(0, 2, 1, 3)
        v = v.reshape(B, N, NUM_KV, HEAD_DIM).transpose(0, 2, 1, 3)
        scores = jnp.einsum('bghnd,bhsd->bghns', q, k)
        attn = jax.nn.softmax(scores / SCALE, axis=-1)
        out = jnp.einsum('bghns,bhsd->bghnd', attn, v)
        out = out.transpose(0, 3, 1, 2, 4).reshape(B, N, NUM_HEADS * HEAD_DIM)
        return out @ Wo + bo

    def _L1_ffn_ref(x, gate_w, Wu, Wv, Wo):
        import jax, jax.numpy as jnp
        import numpy as np
        B, N, D, E, R, K = (4, 512, 256, 8, 64, 2)
        logits = jnp.einsum('bnd,de->bne', x, gate_w)
        topv, topi = jax.lax.top_k(logits, K)
        w = jax.nn.softmax(topv, axis=-1)
        u = jnp.einsum('bnd,edr->bner', x, Wu)
        v = jnp.einsum('bnd,edr->bner', x, Wv)
        s = jax.nn.silu(u) * v
        Y = jnp.einsum('bner,erd->bned', s, Wo)
        y_sel = jnp.take_along_axis(Y, topi[..., None], axis=2)
        out = jnp.einsum('bnkd,bnk->bnd', y_sel, w)
        return out
    x = L0_attn_x
    xn = _layernorm(x, axis=-1)
    x = x + _L0_attn_ref(xn, L0_attn_causal_mask, L0_attn_W_qkv, L0_attn_W_out) + _L0_ffn_ref(xn, L0_ffn_weight, L0_ffn_alpha, L0_ffn_bias)
    xn = _layernorm(x, axis=-1)
    x = x + _L1_attn_ref(xn, L1_attn_Wq, L1_attn_bq, L1_attn_Wk, L1_attn_bk, L1_attn_Wv, L1_attn_bv, L1_attn_Wo, L1_attn_bo) + _L1_ffn_ref(xn, L1_ffn_gate_w, L1_ffn_Wu, L1_ffn_Wv, L1_ffn_Wo)
    return x

_drawn_inputs = setup_inputs


def setup_inputs(seed=0):
    import zlib

    import numpy as np

    out = dict(_drawn_inputs(seed))
    spreads = {'L1_attn_bq': (0.0, 0.8),
     'L1_attn_bk': (0.0, 0.8),
     'L1_attn_bv': (0.0, 0.8),
     'L1_attn_bo': (0.0, 0.8)}
    factors = {'L0_attn_W_qkv': 8.0,
     'L0_attn_W_out': 8.0,
     'L0_ffn_bias': 8.0,
     'L1_attn_Wq': 8.0,
     'L1_attn_Wk': 8.0,
     'L1_attn_Wv': 8.0,
     'L1_attn_Wo': 8.0,
     'L1_ffn_gate_w': 8.0,
     'L1_ffn_Wu': 8.0,
     'L1_ffn_Wv': 8.0,
     'L1_ffn_Wo': 8.0}
    for name, (base, spread) in spreads.items():
        noise = np.random.default_rng([zlib.crc32(name.encode()), seed]).standard_normal(out[name].shape)
        drawn = base * np.exp(spread * noise) if base else spread * noise
        out[name] = jnp.asarray(drawn.astype(out[name].dtype))
    for name, factor in factors.items():
        out[name] = (out[name] * factor).astype(out[name].dtype)
    return out
```

```python
from contextlib import ExitStack

import concourse.bass as bass
from concourse import mybir

F32 = mybir.dt.float32
BF16 = mybir.dt.bfloat16
U32 = mybir.dt.uint32
ALU = mybir.AluOpType
ACT = mybir.ActivationFunctionType
AX_X = mybir.AxisListType.X

P = 128
B, S, D = 4, 2048, 256
H, HD = 16, 16
KV = 4
G = H // KV
E, R = 8, 64
ER = E * R
C = D // P
TILES = S // P
W = 2
PAIRS = TILES // W
QB = 512
QT = S // QB
RB = QB // P
KC = S // P
UNITS = QT * KV * G
SUBS = KC * G
PARTS = 6
ROWS = PARTS * HD
MROW = ROWS
HB = 32
QKV1 = D + 2 * KV * HD
EPS_LN = 1e-5
EPS_DEN = 1e-6
LOADS = 23
CONSTS = 9


def two_layers(nc, x, W_qkv, W_out, W_tern, alpha, bias0, Wq, bq, Wk, bk, Wv, bv, Wo, bo, gate_w, Wu, Wve, Woe, out):
    ctx = ExitStack()
    with ctx:
        def sb(name, shape, dt=F32):
            return ctx.enter_context(nc.sbuf_tensor(name, shape, dt))

        def sem(name):
            return ctx.enter_context(nc.semaphore(name))

        bank = [ctx.enter_context(nc.psum_tensor(f"bank{i}", [P, 512], F32)) for i in range(8)]

        wqkv = sb("wqkv", [P, C, 3 * D])
        wout0 = sb("wout0", [P, KV, D])
        tern_t = sb("tern_t", [P, C, D])
        w1 = sb("w1", [P, C, QKV1 + E])
        wu = sb("wu", [P, C, ER])
        wve = sb("wve", [P, C, ER])
        wout1 = sb("wout1", [P, KV, D])
        woe = sb("woe", [P, ER // P, D])
        bias0_row = sb("bias0_row", [P, D])
        bias1_row = sb("bias1_row", [P, QKV1 + E])
        minus_half = sb("minus_half", [P, 1])
        minus_one = sb("minus_one", [P, RB])
        eps_ln = sb("eps_ln", [P, 1])
        carry = sb("carry", [P, 2 * W])
        carry_v = sb("carry_v", [P, 1])
        spare = sb("spare", [P, 11])
        eps_sum = sb("eps_sum", [P, 1])
        eps_rows = sb("eps_rows", [P, 1])
        alpha_col = sb("alpha_col", [P, 1])
        ones = sb("ones", [P, P])
        tsum = sb("tsum", [P, 1])
        delta = sb("delta", [P, 2])
        ident = sb("ident", [P, P])
        ident_b = sb("ident_b", [P, P], BF16)
        causal = sb("causal", [P, P])
        head_rows = sb("head_rows", [P, 8])
        den_pick = sb("den_pick", [P, G, HB])
        expert_no = sb("expert_no", [P, E])

        qaug = sb("qaug", [P, H, S], BF16)
        kaug = sb("kaug", [P, KV, S], BF16)
        v1 = sb("v1", [P, KC, KV, HB])
        xres = sb("xres", [P, TILES, D])

        def per_tile(name, shape, dt=F32):
            return [sb(f"{name}{j}", shape, dt) for j in range(W)]

        xin = per_tile("xin", [P, D])
        x1 = per_tile("x1", [P, D])
        st6 = per_tile("st6", [P, 6])
        mv = per_tile("mv", [P, 2])
        rstd = per_tile("rstd", [P, 1])
        xn = per_tile("xn", [P, D])
        xnT = per_tile("xnT", [P, C, P])
        phiqT = per_tile("phiqT", [P, C, P])
        phik = per_tile("phik", [P, C, P])
        phiqx = per_tile("phiqx", [P, 8 * P])
        am = per_tile("am", [P, H * P])
        vaug = per_tile("vaug", [P, H, HB])
        state = [sb(f"state{j}", [P, C * 8 * HB]) for j in range(W)]
        osb = per_tile("osb", [P, KV * P])
        xn2T = per_tile("xn2T", [P, C, P])
        qkv = per_tile("qkv", [P, QKV1 + E])
        top8 = per_tile("top8", [P, 8])
        top8i = per_tile("top8i", [P, 8], U32)
        top8f = per_tile("top8f", [P, 8])
        gt = per_tile("gt", [P, 8])
        g1 = per_tile("g1", [P, E])
        g2 = per_tile("g2", [P, E])
        phikT = [xn[j][:].rearrange("p (c q) -> p c q", c=C) for j in range(W)]
        phiqx3 = [phiqx[j][:].rearrange("p (h q) -> p h q", h=8) for j in range(W)]
        am3 = [am[j][:].rearrange("p (h q) -> p h q", h=H) for j in range(W)]
        eu = [am[j][:, 0:ER] for j in range(W)]
        su = [am[j][:, ER:2 * ER] for j in range(W)]
        sT = [am[j][:, 2 * ER:3 * ER].rearrange("p (c q) -> p c q", q=P) for j in range(W)]
        NQK = D + KV * HD
        part = [[am[j][:].bitcast(BF16)[:, 6 * ER + i * NQK:6 * ER + (i + 1) * NQK] for i in range(3)] for j in range(W)]
        qtok = [phiqx[j][:].bitcast(BF16)[:, 0:H * ROWS].rearrange("p (h s d) -> p h s d", h=H, d=HD) for j in range(W)]
        ktok = [phiqx[j][:].bitcast(BF16)[:, H * ROWS:(H + KV) * ROWS].rearrange("p (h s d) -> p h s d", h=KV, d=HD)
                for j in range(W)]

        probs = [phiqx[i // 2][:, (i % 2) * QB:(i % 2 + 1) * QB] for i in range(4)]
        on1 = am[0][:].rearrange("p (g q) -> p g q", g=KV)
        osb1 = osb[0][:]
        ytile = xn
        mx = [sb(f"mx{i}", [P, RB, 4]) for i in range(2)]
        mmax = [sb(f"mmax{i}", [P, RB]) for i in range(2)]
        mrest = sb("mrest", [P, RB])
        mtok = [sb(f"mtok{i}", [P, RB, HB], BF16) for i in range(2)]

        names = """w_small w_all pads filled const total_ps abs_set sum_set delta_set ndelta above tern tern_ps k_rows eps_sum eps_rows
        xb st mv veps veps2 rstd xn xnT_ps xnT q_ps kv_ps negq negk expq expk vaug phiq phik phikT_ps phikT
        phiqx u0_ps um state at_ps am ot_ps osb den_ps on y0_ps x1 st2 mv2 rstd2 xn2 xn2T_ps xn2T prj_ps u_ps ve_ps
        qkv part0 rest part1 part2 qtok_a qtok_p ktok v1 qa_ps qb_ps qa qb kt_ps kt topv topi topf dv edv gsum w1st w2nd
        g1 g2 gw eu eu1 sigm rden rden1 su sv sg sT_ps sT y1_ps xres
        mx_ps mx mmax m1 mrest m2 mT_ps mT s_ps probs av osb1 den1_ps on1 y_ps y""".split()
        s = {n: sem("s_" + n) for n in names}
        s_x_in = [sem(f"s_x_in{j}") for j in range(W)]
        s_st_out = [sem(f"s_st_out{j}") for j in range(W)]

        def bk_(j, i):
            return bank[4 * j + i][:]

        S_BANK, MX_BANK, O_BANK, MT_BANK, DEN_BANK, Y_BANK = (0, 1), (2, 3), 4, 5, 6, 7

        PROBS_RING, S_RING, MX_RING, UNIT_RING = 4, 2, 2, 2
        LEAD = G + 1
        BU = KV * G

        def unit_at(rel, qt):
            return (rel // G) % KV, rel % G, qt + rel // BU

        def tile_numbers(eng, b, p):
            return [eng.snap(b * TILES + p * W + (j + 1)) for j in range(W)]

        block = ctx.enter_context(nc.Block())
        x_flat = x.rearrange("b s d -> (b s) d")
        out_flat = out.rearrange("b s d -> (b s) d")

        @block.sync
        def _(sp):
            n_small = 0
            for dst, src in ((am[0][:, 0:C * D].rearrange("p (c n) -> p c n", c=C), W_tern.rearrange("(c p) n -> p c n", p=P)),
                             (alpha_col[:], alpha.partition_broadcast(P))):
                sp.dma_start(dst, src).then_inc(s["w_small"], 16)
            loads = [(wqkv[:], W_qkv.rearrange("(c p) n -> p c n", p=P)), (bias0_row[:], bias0.partition_broadcast(P))]
            at = 0
            for w, n in ((Wq, D), (Wk, KV * HD), (Wv, KV * HD), (gate_w, E)):
                loads.append((w1[:, :, at:at + n], w.rearrange("(c p) n -> p c n", p=P)))
                at += n
            at = 0
            for w, n in ((bq, D), (bk, KV * HD), (bv, KV * HD)):
                loads.append((bias1_row[:, at:at + n], w.partition_broadcast(P)))
                at += n
            for c in range(C):
                for w, dst in ((Wu, wu), (Wve, wve)):
                    loads.append((dst[:, c, :].rearrange("p (e r) -> p e r", e=E),
                                  w[:, c * P:(c + 1) * P, :].rearrange("e p r -> p e r")))
            loads.append((woe[:], Woe.rearrange("e r n -> (e r) n").rearrange("(c p) n -> p c n", p=P)))
            for dst, src in loads:
                sp.dma_start(dst, src).then_inc(s["w_all"], 16)
            sp.wait_ge(s["pads"], 1)
            padded = [(dst[HB * j:HB * j + HD, :, :], w.rearrange(order, j=G, d=HD)[j])
                      for j in range(G) for w, dst, order in ((W_out, wout0, "(g j d) n -> j d g n"),
                                                              (Wo, wout1, "(j g d) n -> j d g n"))]
            padded.append((wout1[HD:HD + 1, 0, :], bo.rearrange("(a n) -> a n", a=1)))
            for dst, src in padded:
                sp.dma_start(dst, src).then_inc(s["w_all"], 16)
            assert len(loads) + len(padded) == LOADS
            with sp.Fori(0, B) as b:
                with sp.Fori(0, PAIRS) as p:
                    n = tile_numbers(sp, b, p)
                    for j in range(W):
                        sp.wait_ge(s["xb"], n[j])
                        sp.dma_start(xin[j][:], x_flat[bass.ds((n[j] - 1) * P, P), :]).then_inc(s_x_in[j], 16)
                with sp.Fori(0, QT) as qt:
                    for r in range(RB):
                        n = sp.snap(b * TILES + qt * RB + (r + 1))
                        sp.wait_ge(s["y"], n)
                        sp.dma_start(out_flat[bass.ds((n - 1) * P, P), :], ytile[r % W][:]).then_inc(s_st_out[r % W], 16)
            for j in range(W):
                sp.wait_ge(s_st_out[j], 16 * (B * TILES // W + 1))

        @block.gpsimd
        def _(pool):
            g = nc.gpsimd
            g.memset(wout0[:], 0.0)
            g.memset(wout1[:], 0.0)
            g.memset(bias1_row[:, QKV1:QKV1 + E], 0.0).then_inc(s["pads"], 1)
            g.memset(minus_half[:], -0.5).then_inc(s["filled"], 1)
            g.memset(minus_one[:], -1.0).then_inc(s["filled"], 1)
            g.memset(eps_ln[:], EPS_LN).then_inc(s["filled"], 1)
            g.memset(ones[:], 1.0).then_inc(s["filled"], 1)
            g.memset(ident[:], 0.0).then_inc(s["filled"], 1)
            g.memset(ident_b[:], 0.0).then_inc(s["filled"], 1)
            g.memset(causal[:], 1.0).then_inc(s["filled"], 1)
            g.memset(head_rows[:], 1.0).then_inc(s["filled"], 1)
            g.memset(den_pick[:], 0.0).then_inc(s["filled"], 1)
            for j in range(W):
                g.memset(vaug[j][:], 0.0).then_inc(s["filled"], 1)
            g.memset(v1[:], 0.0).then_inc(s["filled"], 1)
            for i in range(2):
                g.memset(mtok[i][:], 0.0).then_inc(s["filled"], 1)
            g.iota(expert_no[:], pattern=[[1, E]], base=0, channel_multiplier=0,
                   allow_small_or_imprecise_dtypes=True).then_inc(s["filled"], 1)
            pool.wait_ge(s["filled"], 15)
            for t in (ident, ident_b):
                g.affine_select(out=t[:], in_=t[:], compare_op=ALU.not_equal, fill=1.0, base=0,
                                pattern=[[-1, P]], channel_multiplier=1).then_inc(s["const"], 1)
            g.affine_select(out=causal[:], in_=causal[:], compare_op=ALU.is_ge, fill=0.0, base=0,
                            pattern=[[1, P]], channel_multiplier=-1).then_inc(s["const"], 1)
            g.affine_select(out=head_rows[:], in_=head_rows[:], compare_op=ALU.is_ge, fill=0.0, base=0,
                            pattern=[[-HD, 8]], channel_multiplier=1).then_inc(s["const"], 1)
            g.affine_select(out=den_pick[:], in_=den_pick[:], compare_op=ALU.not_equal, fill=1.0, base=-HD,
                            pattern=[[-HB, G], [0, HB]], channel_multiplier=1).then_inc(s["const"], 1)
            for j in range(W):
                g.memset(vaug[j][:, :, HD:HD + 1], 1.0).then_inc(s["const"], 1)
            g.memset(v1[:, :, :, HD:HD + 1], 1.0).then_inc(s["const"], 1)
            pool.wait_ge(s["const"], 8)
            g.affine_select(out=head_rows[:], in_=head_rows[:], compare_op=ALU.is_ge, fill=0.0, base=HD - 1,
                            pattern=[[HD, 8]], channel_multiplier=-1).then_inc(s["const"], 1)
            pool.wait_ge(s["const"], CONSTS)
            pool.wait_ge(s["w_all"], 16 * LOADS)
            with pool.Fori(0, B) as b:
                g.memset(state[0][:], 0.0).then_inc(s["state"], 1)
                with pool.Fori(0, PAIRS) as p:
                    n = tile_numbers(pool, b, p)
                    tile0 = pool.snap(p * W)
                    for j in range(W):
                        pool.wait_ge(s["mv"], n[j])
                        g.tensor_tensor(rstd[j][:], mv[j][:, 1:2], eps_ln[:], ALU.add).then_inc(s["veps"], 1)
                    for j in range(W):
                        pool.wait_ge(s["veps"], n[j])
                        g.tensor_tensor(rstd[j][:], rstd[j][:], minus_half[:], ALU.pow).then_inc(s["rstd"], 1)
                    for j in range(W):
                        pool.wait_ge(s["xn"], n[j])
                        g.tensor_tensor(x1[j][:], xin[j][:], bias0_row[:], ALU.add).then_inc(s["xb"], 1)
                    for half in range(C):
                        for j in range(W):
                            if half == 0:
                                pool.wait_ge(s["phiq"], n[j])
                            else:
                                pool.wait_ge(s["at_ps"], (n[0] - 1) * 4 + (2 * j + 2))
                            g.tensor_tensor(phiqx3[j], phiqT[j][:, half, :].unsqueeze(1).broadcast_to([P, 8, P]),
                                            head_rows[:].unsqueeze(2).broadcast_to([P, 8, P]), ALU.mult
                                            ).then_inc(s["phiqx"], 1)
                    pool.wait_ge(s["um"], n[0])
                    g.tensor_tensor(state[1][:], state[0][:], osb[0][:], ALU.add).then_inc(s["state"], 1)
                    pool.wait_ge(s["state"], n[0] + (b + 1))
                    pool.wait_ge(s["um"], n[1])
                    pool.wait_ge(s["ot_ps"], n[0])
                    g.tensor_tensor(state[0][:], state[1][:], osb[1][:], ALU.add).then_inc(s["state"], 1)
                    for j in range(W):
                        pool.wait_ge(s["mv2"], n[j])
                        g.tensor_tensor(rstd[j][:], mv[j][:, 1:2], eps_ln[:], ALU.add).then_inc(s["veps2"], 1)
                    for j in range(W):
                        pool.wait_ge(s["veps2"], n[j])
                        g.tensor_tensor(rstd[j][:], rstd[j][:], minus_half[:], ALU.pow).then_inc(s["rstd2"], 1)
                    for j in range(W):
                        pool.wait_ge(s["part1"], n[j])
                        g.tensor_tensor(carry[:, 2 * j:2 * j + 1], minus_half[:], minus_half[:], ALU.mult)
                        q1 = part[j][1][:, 0:D].rearrange("p (h d) -> p h d", d=HD)
                        k = [part[j][i][:, D:NQK].rearrange("p (h d) -> p h d", d=HD) for i in range(3)]
                        for slot in (3, 4):
                            g.tensor_scalar(qtok[j][:, :, slot, :], q1, 1.0, None, ALU.mult).then_inc(s["qtok_p"], 1)
                        for slot, i in ((0, 0), (3, 0), (5, 0), (1, 1), (4, 1)):
                            g.tensor_scalar(ktok[j][:, :, slot, :], k[i], 1.0, None, ALU.mult)
                        g.tensor_tensor(v1[:, bass.ds(tile0 + j, 1), :, 0:HD],
                                        qkv[j][:, NQK:QKV1].rearrange("p (a h d) -> p a h d", a=1, d=HD),
                                        ones[:, 0:KV * HD].rearrange("p (a h d) -> p a h d", a=1, d=HD), ALU.mult
                                        ).then_inc(s["v1"], 1)
                        pool.wait_ge(s["part2"], n[j])
                        g.tensor_tensor(carry[:, 2 * j + 1:2 * j + 2], minus_half[:], minus_half[:], ALU.mult)
                        g.tensor_scalar(ktok[j][:, :, 2, :], k[2], 1.0, None, ALU.mult).then_inc(s["ktok"], 1)
                    for j in range(W):
                        pool.wait_ge(s["sv"], n[j])
                        pool.wait_ge(s["gw"], n[j])
                        sv = su[j].rearrange("p (e r) -> p e r", e=E)
                        g.tensor_tensor(sv, sv, g1[j][:].unsqueeze(2).broadcast_to([P, E, R]), ALU.mult).then_inc(s["sg"], 1)

                def shift(unit, i):
                    u1 = pool.snap(unit + 1)
                    pool.wait_ge(s["mmax"], u1)
                    pool.wait_ge(s["mT_ps"], u1)
                    g.tensor_tensor(mtok[i][:, :, 0:1], mmax[i][:].unsqueeze(2), minus_one[:].unsqueeze(2), ALU.mult).then_inc(s["m1"], 1)
                    pool.wait_ge(s["m1"], u1)
                    g.tensor_tensor(mrest[:].unsqueeze(2), mmax[i][:].unsqueeze(2), mtok[i][:, :, 0:1], ALU.add
                                    ).then_inc(s["mrest"], 1)
                    pool.wait_ge(s["mrest"], u1)
                    g.tensor_tensor(mtok[i][:, :, 1:2], mrest[:].unsqueeze(2), minus_one[:].unsqueeze(2), ALU.mult).then_inc(s["m2"], 1)

                def block_pool(qt, last):
                    base = (b * QT + qt) * BU
                    for rel in range(LEAD, LEAD + BU):
                        if not (last and rel >= BU):
                            shift(base + rel, rel % 2)

                for rel in range(LEAD):
                    shift(b * UNITS + rel, rel % 2)
                with pool.Fori(0, QT - 1) as qt:
                    block_pool(qt, False)
                block_pool(QT - 1, True)

        @block.scalar
        def _(act):
            a = nc.scalar
            act.wait_ge(s["tern_ps"], 1)
            a.activation(tern_t[:], bk_(0, 0).rearrange("p (c n) -> p c n", c=C), ACT.Copy).then_inc(s["tern"], 1)
            act.wait_ge(s["const"], CONSTS)
            act.wait_ge(s["eps_rows"], 1)
            with act.Fori(0, B) as b:
                with act.Fori(0, PAIRS) as p:
                    n = tile_numbers(act, b, p)
                    for j in range(W):
                        act.wait_ge(s["xnT_ps"], n[j])
                        a.activation(xnT[j][:], bk_(j, 0)[:, 0:D].rearrange("p (c q) -> p c q", c=C), ACT.Copy
                                     ).then_inc(s["xnT"], 1)
                    for j in range(W):
                        act.wait_ge(s["q_ps"], n[j])
                        a.activation(phiqT[j][:], bk_(j, 1)[:, 0:D].rearrange("p (c q) -> p c q", c=C), ACT.Relu, scale=-1.0
                                     ).then_inc(s["negq"], 1)
                        act.wait_ge(s["kv_ps"], n[j])
                        a.activation(phik[j][:], bk_(j, 2)[:, 0:D].rearrange("p (c q) -> p c q", c=C), ACT.Relu, scale=-1.0
                                     ).then_inc(s["negk"], 1)
                        act.wait_ge(s["negq"], n[j])
                        a.activation(phiqT[j][:], phiqT[j][:], ACT.Exp, scale=-1.0).then_inc(s["expq"], 1)
                        act.wait_ge(s["negk"], n[j])
                        a.activation(phik[j][:], phik[j][:], ACT.Exp, scale=-1.0).then_inc(s["expk"], 1)
                        a.activation(vaug[j][:, :, 0:HD], bk_(j, 2)[:, D:2 * D].rearrange("p (h d) -> p h d", d=HD), ACT.Copy
                                     ).then_inc(s["vaug"], 1)
                    for j in range(W):
                        act.wait_ge(s["phikT_ps"], n[j])
                        a.activation(phikT[j], bk_(j, 0)[:, 0:D].rearrange("p (c q) -> p c q", c=C), ACT.Copy
                                     ).then_inc(s["phikT"], 1)
                    for j in range(W):
                        act.wait_ge(s["ot_ps"], n[j])
                        act.wait_ge(s["state"], n[j] + (b + 1))
                        a.activation(osb[j][:], bk_(j, 1), ACT.Identity, bias=eps_rows[:]).then_inc(s["osb"], 1)
                    for j in range(W):
                        act.wait_ge(s["xn2T_ps"], n[j])
                        a.activation(xn2T[j][:], bk_(j, 1)[:, 0:D].rearrange("p (c q) -> p c q", c=C), ACT.Copy
                                     ).then_inc(s["xn2T"], 1)
                    for j in range(W):
                        act.wait_ge(s["u_ps"], n[j])
                        a.activation(eu[j], bk_(j, 3), ACT.Exp, scale=-1.0).then_inc(s["eu"], 1)
                    for j in range(W):
                        act.wait_ge(s["part0"], n[j])
                        a.activation(qtok[j][:, :, 0:3, :],
                                     part[j][0][:, 0:D].rearrange("p (h d) -> p h d", d=HD).unsqueeze(2).broadcast_to([P, H, 3, HD]),
                                     ACT.Copy)
                        act.wait_ge(s["part2"], n[j])
                        a.activation(qtok[j][:, :, 5, :], part[j][2][:, 0:D].rearrange("p (h d) -> p h d", d=HD), ACT.Copy
                                     ).then_inc(s["qtok_a"], 1)
                    for j in range(W):
                        act.wait_ge(s["dv"], n[j])
                        a.activation(gt[j][:, 1:2], gt[j][:, 0:1], ACT.Exp).then_inc(s["edv"], 1)
                    for j in range(W):
                        act.wait_ge(s["sT_ps"], n[j])
                        a.activation(sT[j], bk_(j, 3).rearrange("p (c q) -> p c q", q=P), ACT.Copy).then_inc(s["sT"], 1)

                def shift_rows(unit, g, h, qt):
                    act.wait_ge(s["mT_ps"], unit + (1 + UNIT_RING))
                    a.activation(qaug[MROW:P, G * g + h, bass.ds(qt * QB, QB)],
                                 bank[MT_BANK][MROW:P, 0:QB // 2].bitcast(BF16), ACT.Copy).then_inc(s["mT"], 1)

                def block_act(qt, last):
                    ubase = act.snap((b * QT + qt) * BU)
                    for g in range(KV):
                        grp = act.snap((b * QT + qt) * KV + g)
                        first = act.snap(grp * SUBS)
                        for i in range(SUBS):
                            act.wait_ge(s["s_ps"], first + (i + 1))
                            act.wait_ge(s["av"], first + (i + 1))
                            a.activation(probs[i % PROBS_RING], bank[S_BANK[i % S_RING]][:], ACT.Exp, scale=HD ** -0.5
                                         ).then_inc(s["probs"], 1)
                            if i % 16 == 10:
                                rel = G * g + G + i // 16
                                if not (last and rel >= BU):
                                    shift_rows(ubase + rel, *unit_at(rel, qt))
                        act.wait_ge(s["av"], first + (SUBS + PROBS_RING))
                        if g > 0:
                            act.wait_ge(s["den1_ps"], grp)
                        act.wait_ge(s["on1"], grp + 1)
                        a.activation(osb1, bank[O_BANK][:], ACT.Copy).then_inc(s["osb1"], 1)

                for rel in range(LEAD - 1):
                    shift_rows(b * UNITS + rel, *unit_at(rel, 0))
                with act.Fori(0, QT - 1) as qt:
                    block_act(qt, False)
                block_act(QT - 1, True)

        @block.vector
        def _(dve):
            v = nc.vector
            raw = am[0][:, 0:C * D]
            mag = am[1][:, 0:C * D]
            a_gt = am[0][:, C * D:2 * C * D]
            tern = am[1][:, C * D:2 * C * D]
            dve.wait_ge(s["w_small"], 32)
            v.scalar_tensor_tensor(out=mag, in0=raw, scalar=-1.0, in1=raw, op0=ALU.mult, op1=ALU.max).then_inc(s["abs_set"], 1)
            dve.wait_ge(s["abs_set"], 1)
            v.reduce_sum(tsum[:], mag, AX_X).then_inc(s["sum_set"], 1)
            dve.wait_ge(s["total_ps"], 1)
            v.tensor_scalar(delta[:, 0:1], bk_(0, 1)[:, 0:1], 1.0 / (D * D), 0.7, ALU.mult, ALU.mult).then_inc(s["delta_set"], 1)
            dve.wait_ge(s["delta_set"], 1)
            v.tensor_scalar(delta[:, 1:2], delta[:, 0:1], -1.0, None, ALU.mult).then_inc(s["ndelta"], 1)
            v.tensor_scalar(a_gt, raw, delta[:, 0:1], None, ALU.is_gt).then_inc(s["above"], 1)
            dve.wait_ge(s["ndelta"], 1)
            dve.wait_ge(s["above"], 1)
            v.scalar_tensor_tensor(out=tern, in0=raw, scalar=delta[:, 1:2], in1=a_gt, op0=ALU.is_lt, op1=ALU.subtract,
                                   reverse1=True).then_inc(s["above"], 1)
            dve.wait_ge(s["above"], 2)
            v.tensor_scalar(tern, tern, alpha_col[:], None, ALU.mult).then_inc(s["above"], 1)
            v.memset(kaug[MROW:P, :, :], 0.0).then_inc(s["k_rows"], 1)
            dve.wait_ge(s["k_rows"], 1)
            v.memset(kaug[MROW:MROW + 2, :, :], 1.0).then_inc(s["k_rows"], 1)
            dve.wait_ge(s["const"], CONSTS)
            v.reduce_sum(eps_sum[:], den_pick[:].rearrange("p g e -> p (g e)"), AX_X).then_inc(s["eps_sum"], 1)
            dve.wait_ge(s["eps_sum"], 1)
            v.tensor_scalar(eps_rows[:], eps_sum[:], EPS_DEN / HB, None, ALU.mult).then_inc(s["eps_rows"], 1)
            v.memset(spare[:, 0:1], 0.0).then_inc(s["xb"], W)
            v.memset(spare[:, 1:2], 0.0).then_inc(s["probs"], S_RING)
            v.memset(spare[:, 2:3], 0.0).then_inc(s["av"], PROBS_RING)
            v.memset(spare[:, 3:4], 0.0).then_inc(s["mx"], MX_RING)
            v.memset(spare[:, 4:5], 0.0).then_inc(s["m2"], UNIT_RING)
            v.memset(spare[:, 5:6], 0.0).then_inc(s["mT_ps"], UNIT_RING)
            v.memset(spare[:, 8:9], 0.0).then_inc(s["mT"], 1)
            v.memset(spare[:, 9:10], 0.0).then_inc(s["osb1"], 1)
            v.memset(spare[:, 10:11], 0.0).then_inc(s["on1"], 1)
            for j in range(W):
                v.memset(spare[:, 6 + j:7 + j], 0.0).then_inc(s_st_out[j], 16)
            dve.wait_ge(s["w_all"], 16 * LOADS)

            def norm(j, n, src, k):
                sfx = "" if k == 1 else "2"
                return sfx

            with dve.Fori(0, B) as b:
                with dve.Fori(0, PAIRS) as p:
                    n = tile_numbers(dve, b, p)
                    pair = dve.snap(b * PAIRS + p + 1)
                    tok = [dve.snap(p * (W * P) + j * P) for j in range(W)]

                    def layer_norm(src, st, m, r, done, ready):
                        for j in range(W):
                            ready(j)
                            v.bn_stats(st6[j][:], src[j][:]).then_inc(s[st], 1)
                        dve.wait_ge(s[st], n[W - 1])
                        v.memset(carry_v[:], 0.0)
                        for j in range(W):
                            v.bn_aggr(mv[j][:], st6[j][:]).then_inc(s[m], 1)
                        for j in range(W):
                            dve.wait_ge(s[r], n[j])
                            v.tensor_scalar(xn[j][:], src[j][:], mv[j][:, 0:1], rstd[j][:], ALU.subtract, ALU.mult
                                            ).then_inc(s[done], 1)

                    for j in range(W):
                        dve.wait_ge(s_st_out[j], (b * (TILES // W) + 1) * 16)
                    layer_norm(xin, "st", "mv", "rstd", "xn", lambda j: dve.wait_ge(s_x_in[j], pair * 16))
                    for j in range(W):
                        dve.wait_ge(s["expq"], n[j])
                        v.scalar_tensor_tensor(out=phiqT[j][:].rearrange("p c q -> p (c q)"), in0=bk_(j, 1)[:, 0:D], scalar=1.0,
                                               in1=phiqT[j][:].rearrange("p c q -> p (c q)"), op0=ALU.add, op1=ALU.max
                                               ).then_inc(s["phiq"], 1)
                        dve.wait_ge(s["expk"], n[j])
                        dve.wait_ge(s["vaug"], n[j])
                        v.scalar_tensor_tensor(out=phik[j][:].rearrange("p c q -> p (c q)"), in0=bk_(j, 2)[:, 0:D], scalar=1.0,
                                               in1=phik[j][:].rearrange("p c q -> p (c q)"), op0=ALU.add, op1=ALU.max
                                               ).then_inc(s["phik"], 1)
                    for j in range(W):
                        dve.wait_ge(s["u0_ps"], n[j])
                        v.tensor_tensor(osb[j][:].rearrange("p (c h e) -> p c h e", c=C, h=8),
                                        bk_(j, 3).rearrange("p (c h e) -> p c h e", c=C, h=8),
                                        head_rows[:].unsqueeze(1).unsqueeze(3).broadcast_to([P, C, 8, HB]),
                                        ALU.mult).then_inc(s["um"], 1)
                    for half in range(C):
                        for j in range(W):
                            for q in (2 * half, 2 * half + 1):
                                dve.wait_ge(s["at_ps"], (n[0] - 1) * 4 + (half * 2 * W + 2 * j + q % 2 + 1))
                                v.tensor_tensor(am3[j][:, 4 * q:4 * q + 4, :],
                                                bk_(j, (1, 2, 0, 3)[q]).rearrange("p (h q) -> p h q", h=4),
                                                causal[:].unsqueeze(1).broadcast_to([P, 4, P]), ALU.mult).then_inc(s["am"], 1)
                    for j in range(W):
                        dve.wait_ge(s["den_ps"], n[j])
                        v.reciprocal(eu[j], bk_(j, 2)).then_inc(s["rden"], 1)
                    for j in range(W):
                        dve.wait_ge(s["rden"], n[j])
                        v.tensor_tensor(osb[j][:], osb[j][:], eu[j], ALU.mult).then_inc(s["on"], 1)
                    for j in range(W):
                        dve.wait_ge(s["y0_ps"], n[j])
                        dve.wait_ge(s["xb"], n[j] + W)
                        v.tensor_tensor(x1[j][:], x1[j][:], bk_(j, 0)[:, 0:D], ALU.add).then_inc(s["x1"], 1)
                    layer_norm(x1, "st2", "mv2", "rstd2", "xn2", lambda j: dve.wait_ge(s["x1"], n[j]))
                    for j in range(W):
                        dve.wait_ge(s["prj_ps"], n[j])
                        v.tensor_tensor(qkv[j][:], bk_(j, 2)[:, 0:QKV1 + E], bias1_row[:], ALU.add).then_inc(s["qkv"], 1)
                    for j in range(W):
                        dve.wait_ge(s["qkv"], n[j])
                        v.tensor_copy(part[j][0], qkv[j][:, 0:NQK]).then_inc(s["part0"], 1)
                    for j in range(W):
                        v.max(out=top8[j][:], in_=qkv[j][:, QKV1:QKV1 + E]).then_inc(s["topv"], 1)
                    for j in range(W):
                        dve.wait_ge(s["topv"], n[j])
                        dve.wait_ge(s["part0"], n[j])
                        v.tensor_tensor(qkv[j][:, 0:NQK], qkv[j][:, 0:NQK], part[j][0], ALU.subtract).then_inc(s["rest"], 1)
                    for j in range(W):
                        v.max_index(out=top8i[j][:], in_max=top8[j][:], in_values=qkv[j][:, QKV1:QKV1 + E]).then_inc(s["topi"], 1)
                    for j in range(W):
                        dve.wait_ge(s["rest"], n[j])
                        v.tensor_copy(part[j][1], qkv[j][:, 0:NQK]).then_inc(s["part1"], 1)
                    for j in range(W):
                        v.tensor_tensor(gt[j][:, 0:1], top8[j][:, 1:2], top8[j][:, 0:1], ALU.subtract).then_inc(s["dv"], 1)
                    for j in range(W):
                        dve.wait_ge(s["part1"], n[j])
                        v.tensor_tensor(part[j][2], qkv[j][:, 0:NQK], part[j][1], ALU.subtract).then_inc(s["part2"], 1)
                    for j in range(W):
                        dve.wait_ge(s["topi"], n[j])
                        v.tensor_copy(top8f[j][:], top8i[j][:]).then_inc(s["topf"], 1)
                    for j in range(W):
                        dve.wait_ge(s["eu"], n[j])
                        dve.wait_ge(s["u_ps"], n[j])
                        v.tensor_scalar(eu[j], eu[j], 1.0, None, ALU.add).then_inc(s["eu1"], 1)
                    for j in range(W):
                        dve.wait_ge(s["eu1"], n[j])
                        v.reciprocal(eu[j], eu[j]).then_inc(s["sigm"], 1)
                    for j in range(W):
                        dve.wait_ge(s["sigm"], n[j])
                        v.tensor_tensor(su[j], bk_(j, 3), eu[j], ALU.mult).then_inc(s["su"], 1)
                    for j in range(W):
                        dve.wait_ge(s["edv"], n[j])
                        v.tensor_scalar(gt[j][:, 2:3], gt[j][:, 1:2], 1.0, None, ALU.add).then_inc(s["gsum"], 1)
                    for j in range(W):
                        dve.wait_ge(s["ve_ps"], n[j])
                        dve.wait_ge(s["su"], n[j])
                        v.tensor_tensor(su[j], su[j], bk_(j, 0), ALU.mult).then_inc(s["sv"], 1)
                    for j in range(W):
                        dve.wait_ge(s["gsum"], n[j])
                        v.reciprocal(gt[j][:, 3:4], gt[j][:, 2:3]).then_inc(s["w1st"], 1)
                    for j in range(W):
                        dve.wait_ge(s["w1st"], n[j])
                        v.tensor_tensor(gt[j][:, 4:5], gt[j][:, 3:4], gt[j][:, 1:2], ALU.mult).then_inc(s["w2nd"], 1)
                    for j in range(W):
                        dve.wait_ge(s["topf"], n[j])
                        v.tensor_scalar(g1[j][:], expert_no[:], top8f[j][:, 0:1], gt[j][:, 3:4], ALU.is_equal, ALU.mult
                                        ).then_inc(s["g1"], 1)
                    for j in range(W):
                        dve.wait_ge(s["w2nd"], n[j])
                        v.tensor_scalar(g2[j][:], expert_no[:], top8f[j][:, 1:2], gt[j][:, 4:5], ALU.is_equal, ALU.mult
                                        ).then_inc(s["g2"], 1)
                    for j in range(W):
                        dve.wait_ge(s["g1"], n[j])
                        dve.wait_ge(s["g2"], n[j])
                        v.tensor_tensor(g1[j][:], g1[j][:], g2[j][:], ALU.add).then_inc(s["gw"], 1)
                    for j in range(W):
                        dve.wait_ge(s["qa_ps"], n[j])
                        v.tensor_copy(qaug[0:ROWS, 0:8, bass.ds(tok[j], P)],
                                      bk_(j, 1).bitcast(BF16).rearrange("p (h q) -> p h q", h=8)[0:ROWS]).then_inc(s["qa"], 1)
                        dve.wait_ge(s["qb_ps"], n[j])
                        v.tensor_copy(qaug[0:ROWS, 8:16, bass.ds(tok[j], P)],
                                      bk_(j, 2).bitcast(BF16).rearrange("p (h q) -> p h q", h=8)[0:ROWS]).then_inc(s["qb"], 1)
                    for j in range(W):
                        dve.wait_ge(s["kt_ps"], n[j])
                        v.tensor_copy(kaug[0:ROWS, :, bass.ds(tok[j], P)],
                                      bk_(j, 1).bitcast(BF16)[0:ROWS, 0:KV * P].rearrange("p (h q) -> p h q", h=KV)
                                      ).then_inc(s["kt"], 1)
                    for j in range(W):
                        dve.wait_ge(s["y1_ps"], n[j])
                        v.tensor_tensor(xres[:, bass.ds(p * W + j, 1), :], x1[j][:].unsqueeze(1),
                                        bk_(j, 0)[:, 0:D].unsqueeze(1), ALU.add).then_inc(s["xres"], 1)

                def maxima(first, i, k):
                    dve.wait_ge(s["mx_ps"], first + (k + 1))
                    v.reduce_max(mx[i][:, k // 4, k % 4:k % 4 + 1], bank[MX_BANK[k % MX_RING]][:], AX_X).then_inc(s["mx"], 1)

                def unit_maximum(unit, first, i):
                    dve.wait_ge(s["mx"], first + (16 + MX_RING))
                    dve.wait_ge(s["m2"], unit + 1)
                    v.reduce_max(mmax[i][:], mx[i][:], AX_X).then_inc(s["mmax"], 1)

                def normalize(grp, g):
                    dve.wait_ge(s["den1_ps"], grp + 1)
                    v.reciprocal(on1[:, g, :], bank[DEN_BANK][:]).then_inc(s["rden1"], 1)
                    dve.wait_ge(s["rden1"], grp + 1)
                    v.tensor_tensor(on1[:, g, :], osb1, on1[:, g, :], ALU.mult).then_inc(s["on1"], 1)

                def block_dve(qt, last):
                    base = dve.snap((b * QT + qt) * BU)
                    grp = dve.snap((b * QT + qt) * KV)
                    for g in range(KV):
                        for k in range(G):
                            rel = G * g + LEAD + k
                            valid = not (last and rel >= BU)
                            if valid:
                                first = dve.snap((base + rel) * 16)
                                for kk in range(8):
                                    maxima(first, rel % 2, kk)
                            if k == 0 and g > 0:
                                normalize(grp + (g - 1), g - 1)
                            if valid:
                                for kk in range(8, 16):
                                    maxima(first, rel % 2, kk)
                                unit_maximum(base + rel, first, rel % 2)
                    normalize(grp + (KV - 1), KV - 1)
                    for r in range(RB):
                        t = b * TILES + qt * RB + r
                        dve.wait_ge(s["y_ps"], t + 1)
                        dve.wait_ge(s_st_out[r % W], (b * (TILES // W) + qt * (RB // W) + (r // W + 1)) * 16)
                        v.tensor_tensor(ytile[r % W][:].unsqueeze(1), xres[:, bass.ds(qt * RB + r, 1), :],
                                        bank[(Y_BANK, DEN_BANK)[r % 2]][:, 0:D].unsqueeze(1), ALU.add).then_inc(s["y"], 1)

                for rel in range(LEAD):
                    first = dve.snap((b * UNITS + rel) * 16)
                    for kk in range(16):
                        maxima(first, rel % 2, kk)
                    unit_maximum(b * UNITS + rel, first, rel % 2)
                with dve.Fori(0, QT - 1) as qt:
                    block_dve(qt, False)
                block_dve(QT - 1, True)

        @block.tensor
        def _(pe):
            t = nc.tensor
            mm = t.matmul
            pe.wait_ge(s["const"], CONSTS)
            pe.wait_ge(s["sum_set"], 1)
            mm(bk_(0, 1)[:, 0:1], ones[:], tsum[:], start=True, stop=True).then_inc(s["total_ps"], 1)
            pe.wait_ge(s["above"], 3)
            for c in range(C):
                for o in range(C):
                    last = t.transpose(bk_(0, 0)[:, c * D + o * P:c * D + (o + 1) * P],
                                       am[1][:, C * D + o * D + c * P:C * D + o * D + (c + 1) * P], ident[:])
            last.then_inc(s["tern_ps"], 1)
            pe.wait_ge(s["w_all"], 16 * LOADS)
            pe.wait_ge(s["tern"], 1)
            pe.wait_ge(s["k_rows"], 2)
            with pe.Fori(0, B) as b:
                with pe.Fori(0, PAIRS) as p:
                    n = tile_numbers(pe, b, p)
                    for j in range(W):
                        pe.wait_ge(s["xn"], n[j])
                        for c in range(C):
                            last = t.transpose(bk_(j, 0)[:, c * P:(c + 1) * P], xn[j][:, c * P:(c + 1) * P], ident[:])
                        last.then_inc(s["xnT_ps"], 1)
                    for j in range(W):
                        pe.wait_ge(s["xnT"], n[j])
                        for m in range(C):
                            for c in range(C):
                                last = mm(bk_(j, 1)[:, m * P:(m + 1) * P], wqkv[:, c, m * P:(m + 1) * P], xnT[j][:, c, :],
                                          start=c == 0, stop=c == C - 1)
                        last.then_inc(s["q_ps"], 1)
                        for c in range(C):
                            last = mm(bk_(j, 2), xnT[j][:, c, :], wqkv[:, c, D:3 * D], start=c == 0, stop=c == C - 1)
                        last.then_inc(s["kv_ps"], 1)
                    for j in range(W):
                        pe.wait_ge(s["phik"], n[j])
                        for c in range(C):
                            last = t.transpose(bk_(j, 0)[:, c * P:(c + 1) * P], phik[j][:, c, :], ident[:])
                        last.then_inc(s["phikT_ps"], 1)
                        pe.wait_ge(s["vaug"], n[j])
                        for c in range(C):
                            last = mm(bk_(j, 3)[:, c * D:(c + 1) * D], phik[j][:, c, :],
                                      vaug[j][:, 8 * c:8 * c + 8, :].rearrange("p h e -> p (h e)"), start=True, stop=True)
                        last.then_inc(s["u0_ps"], 1)
                    for half in range(C):
                        for j in range(W):
                            pe.wait_ge(s["phikT"], n[j])
                            pe.wait_ge(s["phiqx"], (n[j] - (j + 1)) * 2 + (half * W + j + 1))
                            for q in (2 * half, 2 * half + 1):
                                if q == 3:
                                    pe.wait_ge(s["um"], n[j])
                                mm(bk_(j, (1, 2, 0, 3)[q]), phikT[j][:, half, :],
                                   phiqx[j][:, (q % 2) * 512:(q % 2 + 1) * 512], start=True, stop=True).then_inc(s["at_ps"], 1)
                    for j in range(W):
                        pe.wait_ge(s["am"], (n[0] - 1) * 4 + (2 * W + 2 * j + 2))
                        pe.wait_ge(s["state"], n[j] + b)
                        for g in range(KV):
                            mm(bk_(j, 1)[:, g * P:(g + 1) * P], state[j][:, g * P:(g + 1) * P], phiqT[j][:, g // 2, :],
                               start=True, stop=False, skip_group_check=True)
                            for h in range(G):
                                last = mm(bk_(j, 1)[HB * h:HB * (h + 1), g * P:(g + 1) * P], vaug[j][:, G * g + h, :],
                                          am3[j][:, G * g + h, :], start=False, stop=True, skip_group_check=True)
                        last.then_inc(s["ot_ps"], 1)
                    for j in range(W):
                        pe.wait_ge(s["osb"], n[j])
                        mm(bk_(j, 2), den_pick[:].rearrange("p g e -> p (g e)"), osb[j][:], start=True, stop=True
                           ).then_inc(s["den_ps"], 1)
                    for j in range(W):
                        for c in range(C):
                            mm(bk_(j, 0)[:, 0:D], xnT[j][:, c, :], tern_t[:, c, :], start=c == 0, stop=False)
                        pe.wait_ge(s["on"], n[j])
                        for g in range(KV):
                            last = mm(bk_(j, 0)[:, 0:D], osb[j][:, g * P:(g + 1) * P], wout0[:, g, :], start=False, stop=g == KV - 1)
                        last.then_inc(s["y0_ps"], 1)
                    for j in range(W):
                        pe.wait_ge(s["xn2"], n[j])
                        for c in range(C):
                            last = t.transpose(bk_(j, 1)[:, c * P:(c + 1) * P], xn[j][:, c * P:(c + 1) * P], ident[:])
                        last.then_inc(s["xn2T_ps"], 1)
                    for j in range(W):
                        pe.wait_ge(s["xn2T"], n[j])
                        for c in range(C):
                            last = mm(bk_(j, 2)[:, 0:QKV1 + E], xn2T[j][:, c, :], w1[:, c, :], start=c == 0, stop=c == C - 1)
                        last.then_inc(s["prj_ps"], 1)
                    for j in range(W):
                        for w, dst, sm in ((wu, 3, "u_ps"), (wve, 0, "ve_ps")):
                            for c in range(C):
                                last = mm(bk_(j, dst), xn2T[j][:, c, :], w[:, c, :], start=c == 0, stop=c == C - 1)
                            last.then_inc(s[sm], 1)

                    def to_rows(j, bank_, tok, heads):
                        dst = bk_(j, bank_).bitcast(BF16)
                        for i, h in enumerate(heads):
                            last = t.transpose(dst[0:ROWS, i * P:(i + 1) * P], tok[j][:, h, 0:PARTS, :].rearrange("p s d -> p (s d)"),
                                               ident_b[:])
                        return last

                    for j in range(W):
                        pe.wait_ge(s["qtok_a"], n[j])
                        pe.wait_ge(s["qtok_p"], n[j] * 2)
                        to_rows(j, 1, qtok, range(0, 8)).then_inc(s["qa_ps"], 1)
                        pe.wait_ge(s["part0"], n[j])
                        to_rows(j, 2, qtok, range(8, 16)).then_inc(s["qb_ps"], 1)
                    for j in range(W):
                        pe.wait_ge(s["ktok"], n[j])
                        pe.wait_ge(s["qa"], n[j])
                        to_rows(j, 1, ktok, range(KV)).then_inc(s["kt_ps"], 1)
                    for j in range(W):
                        pe.wait_ge(s["sg"], n[j])
                        for c in range(ER // P):
                            last = t.transpose(bk_(j, 3)[:, c * P:(c + 1) * P], su[j][:, c * P:(c + 1) * P], ident[:])
                        last.then_inc(s["sT_ps"], 1)
                    for j in range(W):
                        pe.wait_ge(s["sT"], n[j])
                        for c in range(ER // P):
                            last = mm(bk_(j, 0)[:, 0:D], sT[j][:, c, :], woe[:, c, :], start=c == 0, stop=c == ER // P - 1)
                        last.then_inc(s["y1_ps"], 1)

                def maxima(first, gg, h, qt, k):
                    pe.wait_ge(s["mx"], first + (k + 1))
                    mm(bank[MX_BANK[k % MX_RING]][:], qaug[0:ROWS, G * gg + h, bass.ds(qt * QB + (k // 4) * P, P)],
                       kaug[0:ROWS, gg, (k % 4) * 512:(k % 4 + 1) * 512], start=True, stop=True).then_inc(s["mx_ps"], 1)

                def shift_rows(unit, i):
                    pe.wait_ge(s["m2"], unit + (1 + UNIT_RING))
                    pe.wait_ge(s["mT"], unit + 1)
                    for r in range(RB):
                        last = t.transpose(bank[MT_BANK][MROW:P, r * (P // 2):(r + 1) * (P // 2)].bitcast(BF16), mtok[i][:, r, :],
                                           ident_b[:])
                    last.then_inc(s["mT_ps"], 1)

                def denominators(grp):
                    pe.wait_ge(s["osb1"], grp + 2)
                    mm(bank[DEN_BANK][:], den_pick[:].rearrange("p g e -> p (g e)"), osb1, start=True, stop=True
                       ).then_inc(s["den1_ps"], 1)

                def block_pe(qt, last_block):
                    base = pe.snap((b * QT + qt) * BU)
                    grp0 = pe.snap((b * QT + qt) * KV)

                    def weighted(first, g, i):
                        h, kc = i % G, i // G
                        pe.wait_ge(s["probs"], first + (i + 1 + S_RING))
                        return mm(bank[O_BANK][HB * h:HB * (h + 1), :], v1[:, kc, g, :], probs[i % PROBS_RING],
                                  start=kc == 0, stop=kc == KC - 1, skip_group_check=True).then_inc(s["av"], 1)

                    for g in range(KV):
                        first = pe.snap((grp0 + g) * SUBS)
                        for i in range(SUBS):
                            h, kc = i % G, i // G
                            if kc == 0:
                                pe.wait_ge(s["mT"], base + (G * g + h + 2))
                            pe.wait_ge(s["probs"], first + (i + 1))
                            mm(bank[S_BANK[i % S_RING]][:], kaug[:, g, kc * P:(kc + 1) * P],
                               qaug[:, G * g + h, bass.ds(qt * QB, QB)], start=True, stop=True).then_inc(s["s_ps"], 1)
                            rel = G * g + LEAD + i // 16
                            if not (last_block and rel >= BU):
                                if i % 16 == 0:
                                    mfirst = pe.snap((base + rel) * 16)
                                maxima(mfirst, *unit_at(rel, qt), i % 16)
                            if i == 2:
                                pe.wait_ge(s["osb1"], grp0 + (g + 1))
                            if i >= 2:
                                weighted(first, g, i - 2)
                            if i % 16 == 8:
                                rel = G * g + G + i // 16
                                if not (last_block and rel >= BU):
                                    shift_rows(base + rel, rel % 2)
                            if i == 5 and g > 0:
                                denominators(grp0 + (g - 1))
                        weighted(first, g, SUBS - 2)
                        weighted(first, g, SUBS - 1)
                    denominators(grp0 + (KV - 1))
                    for r in range(RB):
                        tile = b * TILES + qt * RB + r
                        pe.wait_ge(s["on1"], grp0 + (KV + 1))
                        if r >= 2:
                            pe.wait_ge(s["y"], tile - 1)
                        for g in range(KV):
                            last = mm(bank[(Y_BANK, DEN_BANK)[r % 2]][:, 0:D], on1[:, g, r * P:(r + 1) * P], wout1[:, g, :],
                                      start=g == 0, stop=g == KV - 1)
                        last.then_inc(s["y_ps"], 1)

                pe.wait_ge(s["xres"], (b + 1) * TILES)
                pe.wait_ge(s["v1"], (b + 1) * TILES)
                for rel in range(LEAD):
                    first = pe.snap((b * UNITS + rel) * 16)
                    for k in range(16):
                        maxima(first, *unit_at(rel, 0), k)
                    if rel >= 1:
                        shift_rows(b * UNITS + (rel - 1), (rel - 1) % 2)
                with pe.Fori(0, QT - 1) as qt:
                    block_pe(qt, False)
                block_pe(QT - 1, True)

    return nc


_INS = ["L0_attn_x", "L0_attn_W_qkv", "L0_attn_W_out", "L0_ffn_weight", "L0_ffn_alpha", "L0_ffn_bias",
        "L1_attn_Wq", "L1_attn_bq", "L1_attn_Wk", "L1_attn_bk", "L1_attn_Wv", "L1_attn_bv", "L1_attn_Wo", "L1_attn_bo",
        "L1_ffn_gate_w", "L1_ffn_Wu", "L1_ffn_Wv", "L1_ffn_Wo"]


def kernel(**inputs):
    import numpy as _np
    import concourse.bacc as _bacc
    from concourse import mybir as _mybir
    from concourse.bass_utils import run_bass_kernel_spmd as _run

    nc = _bacc.Bacc("TRN2", target_bir_lowering=False, num_devices=1)
    arrays, args = {}, []
    for name in _INS:
        a = _np.ascontiguousarray(inputs[name])
        arrays[f"in_{name}_dram"] = a
        args.append(nc.dram_tensor(f"in_{name}_dram", a.shape, _mybir.dt.from_np(a.dtype), kind="ExternalInput").ap())
    args.append(nc.dram_tensor("out_0_dram", (B, S, D), _mybir.dt.float32, kind="ExternalOutput").ap())
    two_layers(nc, *args)
    r = _run(nc, [arrays], core_ids=[0])
    return r.results[0]["out_0_dram"]
```

```python
from contextlib import ExitStack

import concourse.bass as bass
from concourse import mybir

F32 = mybir.dt.float32
BF16 = mybir.dt.bfloat16
U32 = mybir.dt.uint32
ALU = mybir.AluOpType
ACT = mybir.ActivationFunctionType
AX_X = mybir.AxisListType.X

P = 128
B, S, D = 4, 2048, 256
H, HD = 16, 16
KV = 4
G = H // KV
E, R = 8, 64
ER = E * R
C = D // P
TILES = S // P
W = 2
PAIRS = TILES // W
QB = 512
QT = S // QB
RB = QB // P
KC = S // P
UNITS = QT * KV * G
SUBS = KC * G
PARTS = 6
ROWS = PARTS * HD
MROW = ROWS
HB = 32
QKV1 = D + 2 * KV * HD
EPS_LN = 1e-5
EPS_DEN = 1e-6
LOADS = 17
CONSTS = 9


def two_layers(nc, x, W_qkv, W_out, W_tern, alpha, bias0, Wq, bq, Wk, bk, Wv, bv, Wo, bo, gate_w, Wu, Wve, Woe, out):
    ctx = ExitStack()
    with ctx:
        def sb(name, shape, dt=F32):
            return ctx.enter_context(nc.sbuf_tensor(name, shape, dt))

        def sem(name):
            return ctx.enter_context(nc.semaphore(name))

        bank = [ctx.enter_context(nc.psum_tensor(f"bank{i}", [P, 512], F32)) for i in range(8)]

        wqkv = sb("wqkv", [P, C, 3 * D])
        wout0 = sb("wout0", [P, C, D])
        tern_t = sb("tern_t", [P, C, D])
        w1 = sb("w1", [P, C, QKV1 + E])
        wu = sb("wu", [P, C, ER])
        wve = sb("wve", [P, C, ER])
        wout1 = sb("wout1", [P, C, D])
        woe = sb("woe", [P, ER // P, D])
        bias0_row = sb("bias0_row", [P, D])
        bo_row = sb("bo_row", [P, D])
        bias1_row = sb("bias1_row", [P, QKV1 + E])
        minus_half = sb("minus_half", [P, 1])
        minus_one = sb("minus_one", [P, RB])
        eps_ln = sb("eps_ln", [P, 1])
        carry = sb("carry", [P, 2 * W])
        carry_v = sb("carry_v", [P, 1])
        spare = sb("spare", [P, 14])
        eps_rows = sb("eps_rows", [P, 1])
        alpha_col = sb("alpha_col", [P, 1])
        ones = sb("ones", [P, P])
        tsum = sb("tsum", [P, 1])
        delta = sb("delta", [P, 2])
        ident = sb("ident", [P, P])
        ident_b = sb("ident_b", [P, P], BF16)
        causal = sb("causal", [P, P])
        head_rows = sb("head_rows", [P, 8])
        eps_pick = sb("eps_pick", [P, G])
        expert_no = sb("expert_no", [P, E])

        qaug = sb("qaug", [P, H, S], BF16)
        kaug = sb("kaug", [P, KV, S], BF16)
        v1 = sb("v1", [P, KC, KV, HB])
        xres = sb("xres", [P, TILES, D])

        def per_tile(name, shape, dt=F32):
            return [sb(f"{name}{j}", shape, dt) for j in range(W)]

        xin = per_tile("xin", [P, D])
        x1 = per_tile("x1", [P, D])
        st6 = per_tile("st6", [P, 6])
        mv = per_tile("mv", [P, 2])
        rstd = per_tile("rstd", [P, 1])
        xn = per_tile("xn", [P, D])
        xnT = per_tile("xnT", [P, C, P])
        phiqT = per_tile("phiqT", [P, C, P])
        phik = per_tile("phik", [P, C, P])
        phiqx = per_tile("phiqx", [P, 8 * P])
        am = per_tile("am", [P, H * P])
        vaug = per_tile("vaug", [P, H, HB])
        state = [sb(f"state{j}", [P, C * 8 * HB]) for j in range(W)]
        osb = per_tile("osb", [P, KV * P])
        xn2T = per_tile("xn2T", [P, C, P])
        qkv = per_tile("qkv", [P, QKV1 + E])
        top8 = per_tile("top8", [P, 8])
        top8i = per_tile("top8i", [P, 8], U32)
        top8f = per_tile("top8f", [P, 8])
        gt = per_tile("gt", [P, 8])
        rden = per_tile("rden", [P, H])
        g1 = per_tile("g1", [P, E])
        g2 = per_tile("g2", [P, E])
        phikT = [xn[j][:].rearrange("p (c q) -> p c q", c=C) for j in range(W)]
        phiqx3 = [phiqx[j][:].rearrange("p (h q) -> p h q", h=8) for j in range(W)]
        am3 = [am[j][:].rearrange("p (h q) -> p h q", h=H) for j in range(W)]
        eu = [am[j][:, 0:ER] for j in range(W)]
        on0 = [am[j][:, 0:D].rearrange("p (h d) -> p h d", d=HD) for j in range(W)]
        on0T = [osb[j][:, 0:D].rearrange("p (c q) -> p c q", c=C) for j in range(W)]
        su = [am[j][:, ER:2 * ER] for j in range(W)]
        sT = [am[j][:, 2 * ER:3 * ER].rearrange("p (c q) -> p c q", q=P) for j in range(W)]
        NQK = D + KV * HD
        part = [[am[j][:].bitcast(BF16)[:, 6 * ER + i * NQK:6 * ER + (i + 1) * NQK] for i in range(3)] for j in range(W)]
        qtok = [phiqx[j][:].bitcast(BF16)[:, 0:H * ROWS].rearrange("p (h s d) -> p h s d", h=H, d=HD) for j in range(W)]
        ktok = [phiqx[j][:].bitcast(BF16)[:, H * ROWS:(H + KV) * ROWS].rearrange("p (h s d) -> p h s d", h=KV, d=HD)
                for j in range(W)]

        probs = [(phiqx[0], phiqx[1], am[1])[min(i // 2, 2)][:, (i % 2 if i < 4 else i - 4) * QB:(i % 2 + 1 if i < 4 else i - 3) * QB]
                 for i in range(2 * G)]
        on1 = am[0][:, 0:RB * D].rearrange("p (r n) -> p r n", r=RB)
        on1T = am[0][:, RB * D:2 * RB * D].rearrange("p (r c q) -> p r c q", r=RB, c=C)
        osb1 = osb[0][:]
        rden1 = sb("rden_1", [P, RB, G])
        ytile = xn
        mx = [sb(f"mx{i}", [P, RB, 4]) for i in range(2)]
        mmax = [sb(f"mmax{i}", [P, RB]) for i in range(2)]
        mrest = sb("mrest", [P, RB])
        mtok = [sb(f"mtok{i}", [P, RB, HB], BF16) for i in range(2)]

        names = """w_small w_all filled const total_ps abs_set sum_set delta_set ndelta above tern tern_ps k_rows eps_rows
        xb st mv veps veps2 rstd xn xnT_ps xnT q_ps kv_ps negq negk expq expk vaug phiq phik phikT_ps phikT
        phiqx u0_ps um state at_ps am ot_ps osb den_ps rden on onT_ps onT y0_ps x1 st2 mv2 rstd2 xn2 xn2T_ps xn2T prj_ps u_ps ve_ps
        qkv part0 rest part1 part2 qtok_a qtok_p ktok v1 qa_ps qb_ps qa qb kt_ps kt topv topi topf dv edv gsum w1st w2nd
        g1 g2 gw tu su sv x1b sg sT_ps sT y1_ps xres
        mx_ps mx mmax m1 mrest m2 mT_ps mT s_ps probs av osb1 out_ps rden1 on1 turn_ps turn y_ps y""".split()
        s = {n: sem("s_" + n) for n in names}
        s_x_in = [sem(f"s_x_in{j}") for j in range(W)]
        s_st_out = [sem(f"s_st_out{j}") for j in range(W)]

        def bk_(j, i):
            return bank[4 * j + i][:]

        S_BANK, MX_BANK, O_BANK, MISC_BANK = (0, 1), (2, 3, 4, 5), 6, 7

        AV_AFTER, MAXIMA_AFTER = 1, ((0,), (), (), (1, 2, 3))
        OUT_AT, TURN_AT, PROJ_AT, SHIFT_AT = 1, (3, 4), (7, 8, 9, 11), (2, 6, 10, 14)

        PROBS_RING, S_RING, MX_RING, UNIT_RING = 2, 2, 4, 2
        LEAD = G + 1
        BU = KV * G

        def unit_at(rel, qt):
            return (rel // G) % KV, rel % G, qt + rel // BU

        def tile_numbers(eng, b, p):
            return [eng.snap(b * TILES + p * W + (j + 1)) for j in range(W)]


        block = ctx.enter_context(nc.Block())
        x_flat = x.rearrange("b s d -> (b s) d")
        out_flat = out.rearrange("b s d -> (b s) d")

        @block.sync
        def _(sp):
            for dst, src in ((am[0][:, 0:C * D].rearrange("p (c n) -> p c n", c=C), W_tern.rearrange("(c p) n -> p c n", p=P)),
                             (alpha_col[:], alpha.partition_broadcast(P))):
                sp.dma_start(dst, src).then_inc(s["w_small"], 16)
            loads = [(wqkv[:], W_qkv.rearrange("(c p) n -> p c n", p=P)), (bias0_row[:], bias0.partition_broadcast(P)),
                     (bo_row[:], bo.partition_broadcast(P)), (wout0[:], W_out.rearrange("(c p) n -> p c n", p=P)),
                     (wout1[:], Wo.rearrange("(c p) n -> p c n", p=P))]
            at = 0
            for w, n in ((Wq, D), (Wk, KV * HD), (Wv, KV * HD), (gate_w, E)):
                loads.append((w1[:, :, at:at + n], w.rearrange("(c p) n -> p c n", p=P)))
                at += n
            at = 0
            for w, n in ((bq, D), (bk, KV * HD), (bv, KV * HD)):
                loads.append((bias1_row[:, at:at + n], w.partition_broadcast(P)))
                at += n
            for c in range(C):
                for w, dst in ((Wu, wu), (Wve, wve)):
                    loads.append((dst[:, c, :].rearrange("p (e r) -> p e r", e=E),
                                  w[:, c * P:(c + 1) * P, :].rearrange("e p r -> p e r")))
            loads.append((woe[:], Woe.rearrange("e r n -> (e r) n").rearrange("(c p) n -> p c n", p=P)))
            for dst, src in loads:
                sp.dma_start(dst, src).then_inc(s["w_all"], 16)
            assert len(loads) == LOADS
            with sp.Fori(0, B) as b:
                with sp.Fori(0, PAIRS) as p:
                    n = tile_numbers(sp, b, p)
                    for j in range(W):
                        sp.wait_ge(s["xb"], n[j])
                        sp.dma_start(xin[j][:], x_flat[bass.ds((n[j] - 1) * P, P), :]).then_inc(s_x_in[j], 16)
                with sp.Fori(0, QT) as qt:
                    for r in range(RB):
                        n = sp.snap(b * TILES + qt * RB + (r + 1))
                        sp.wait_ge(s["y"], n + 1)
                        sp.dma_start(out_flat[bass.ds((n - 1) * P, P), :], ytile[r % W][:]).then_inc(s_st_out[r % W], 16)
            for j in range(W):
                sp.wait_ge(s_st_out[j], 16 * (B * TILES // W + 1))

        @block.gpsimd
        def _(pool):
            g = nc.gpsimd
            g.memset(bias1_row[:, QKV1:QKV1 + E], 0.0).then_inc(s["filled"], 1)
            g.memset(minus_half[:], -0.5).then_inc(s["filled"], 1)
            g.memset(minus_one[:], -1.0).then_inc(s["filled"], 1)
            g.memset(eps_ln[:], EPS_LN).then_inc(s["filled"], 1)
            g.memset(ones[:], 1.0).then_inc(s["filled"], 1)
            g.memset(ident[:], 0.0).then_inc(s["filled"], 1)
            g.memset(ident_b[:], 0.0).then_inc(s["filled"], 1)
            g.memset(causal[:], 1.0).then_inc(s["filled"], 1)
            g.memset(head_rows[:], 1.0).then_inc(s["filled"], 1)
            g.memset(eps_pick[:], 0.0).then_inc(s["filled"], 1)
            for j in range(W):
                g.memset(vaug[j][:], 0.0).then_inc(s["filled"], 1)
            g.memset(v1[:], 0.0).then_inc(s["filled"], 1)
            for i in range(2):
                g.memset(mtok[i][:], 0.0).then_inc(s["filled"], 1)
            g.iota(expert_no[:], pattern=[[1, E]], base=0, channel_multiplier=0,
                   allow_small_or_imprecise_dtypes=True).then_inc(s["filled"], 1)
            pool.wait_ge(s["filled"], 16)
            for t in (ident, ident_b):
                g.affine_select(out=t[:], in_=t[:], compare_op=ALU.not_equal, fill=1.0, base=0,
                                pattern=[[-1, P]], channel_multiplier=1).then_inc(s["const"], 1)
            g.affine_select(out=causal[:], in_=causal[:], compare_op=ALU.is_ge, fill=0.0, base=0,
                            pattern=[[1, P]], channel_multiplier=-1).then_inc(s["const"], 1)
            g.affine_select(out=head_rows[:], in_=head_rows[:], compare_op=ALU.is_ge, fill=0.0, base=0,
                            pattern=[[-HD, 8]], channel_multiplier=1).then_inc(s["const"], 1)
            g.affine_select(out=eps_pick[:], in_=eps_pick[:], compare_op=ALU.not_equal, fill=EPS_DEN, base=-HD,
                            pattern=[[-HB, G]], channel_multiplier=1).then_inc(s["const"], 1)
            for j in range(W):
                g.memset(vaug[j][:, :, HD:HD + 1], 1.0).then_inc(s["const"], 1)
            g.memset(v1[:, :, :, HD:HD + 1], 1.0).then_inc(s["const"], 1)
            pool.wait_ge(s["const"], 8)
            g.affine_select(out=head_rows[:], in_=head_rows[:], compare_op=ALU.is_ge, fill=0.0, base=HD - 1,
                            pattern=[[HD, 8]], channel_multiplier=-1).then_inc(s["const"], 1)
            pool.wait_ge(s["const"], CONSTS)
            pool.wait_ge(s["w_all"], 16 * LOADS)
            with pool.Fori(0, B) as b:
                g.memset(state[0][:], 0.0).then_inc(s["state"], 1)
                def front_pool(n):
                    for j in range(W):
                        pool.wait_ge(s["mv"], n[j])
                        g.tensor_tensor(rstd[j][:], mv[j][:, 1:2], eps_ln[:], ALU.add).then_inc(s["veps"], 1)
                    for j in range(W):
                        pool.wait_ge(s["veps"], n[j])
                        g.tensor_tensor(rstd[j][:], rstd[j][:], minus_half[:], ALU.pow).then_inc(s["rstd"], 1)

                def rest_pool(p, more):
                    n = tile_numbers(pool, b, p)
                    tile0 = pool.snap(p * W)
                    for half in range(C):
                        for j in range(W):
                            if half == 0:
                                pool.wait_ge(s["phiq"], n[j])
                                pool.wait_ge(s["kt"], n[j])
                            else:
                                pool.wait_ge(s["at_ps"], (n[0] - 1) * 4 + (2 * j + 2))
                            g.tensor_tensor(phiqx3[j], phiqT[j][:, half, :].unsqueeze(1).broadcast_to([P, 8, P]),
                                            head_rows[:].unsqueeze(2).broadcast_to([P, 8, P]), ALU.mult
                                            ).then_inc(s["phiqx"], 1)
                    pool.wait_ge(s["um"], n[0])
                    g.tensor_tensor(state[1][:], state[0][:], osb[0][:], ALU.add).then_inc(s["state"], 1)
                    pool.wait_ge(s["state"], n[0] + (b + 1))
                    pool.wait_ge(s["um"], n[1])
                    pool.wait_ge(s["ot_ps"], n[0])
                    g.tensor_tensor(state[0][:], state[1][:], osb[1][:], ALU.add).then_inc(s["state"], 1)
                    for j in range(W):
                        g.tensor_tensor(x1[j][:], xin[j][:], bias0_row[:], ALU.add).then_inc(s["xb"], 1)
                    for j in range(W):
                        pool.wait_ge(s["mv2"], n[j])
                        g.tensor_tensor(rstd[j][:], mv[j][:, 1:2], eps_ln[:], ALU.add).then_inc(s["veps2"], 1)
                        pool.wait_ge(s["veps2"], n[j])
                        g.tensor_tensor(rstd[j][:], rstd[j][:], minus_half[:], ALU.pow).then_inc(s["rstd2"], 1)
                    if more:
                        front_pool(tile_numbers(pool, b, p + 1))
                    for j in range(W):
                        pool.wait_ge(s["xn2"], n[j])
                        g.tensor_tensor(x1[j][:], x1[j][:], bo_row[:], ALU.add).then_inc(s["x1b"], 1)
                    for j in range(W):
                        pool.wait_ge(s["part1"], n[j])
                        g.tensor_tensor(carry[:, 2 * j:2 * j + 1], minus_half[:], minus_half[:], ALU.mult)
                        q1 = part[j][1][:, 0:D].rearrange("p (h d) -> p h d", d=HD)
                        k = [part[j][i][:, D:NQK].rearrange("p (h d) -> p h d", d=HD) for i in range(3)]
                        for slot in (3, 4):
                            g.tensor_scalar(qtok[j][:, :, slot, :], q1, 1.0, None, ALU.mult).then_inc(s["qtok_p"], 1)
                        for slot, i in ((0, 0), (3, 0), (5, 0), (1, 1), (4, 1)):
                            g.tensor_scalar(ktok[j][:, :, slot, :], k[i], 1.0, None, ALU.mult)
                        g.tensor_tensor(v1[:, bass.ds(tile0 + j, 1), :, 0:HD],
                                        qkv[j][:, NQK:QKV1].rearrange("p (a h d) -> p a h d", a=1, d=HD),
                                        ones[:, 0:KV * HD].rearrange("p (a h d) -> p a h d", a=1, d=HD), ALU.mult
                                        ).then_inc(s["v1"], 1)
                        pool.wait_ge(s["part2"], n[j])
                        g.tensor_tensor(carry[:, 2 * j + 1:2 * j + 2], minus_half[:], minus_half[:], ALU.mult)
                        g.tensor_scalar(ktok[j][:, :, 2, :], k[2], 1.0, None, ALU.mult).then_inc(s["ktok"], 1)
                    for j in range(W):
                        pool.wait_ge(s["sv"], n[j])
                        pool.wait_ge(s["gw"], n[j])
                        sv = su[j].rearrange("p (e r) -> p e r", e=E)
                        g.tensor_tensor(sv, sv, g1[j][:].unsqueeze(2).broadcast_to([P, E, R]), ALU.mult).then_inc(s["sg"], 1)

                front_pool(tile_numbers(pool, b, 0))
                with pool.Fori(0, PAIRS - 1) as p:
                    rest_pool(p, True)
                rest_pool(PAIRS - 1, False)

                def shift(unit, i):
                    u1 = pool.snap(unit + 1)
                    pool.wait_ge(s["mmax"], u1)
                    pool.wait_ge(s["mT_ps"], u1)
                    g.tensor_tensor(mtok[i][:, :, 0:1], mmax[i][:].unsqueeze(2), minus_one[:].unsqueeze(2), ALU.mult).then_inc(s["m1"], 1)
                    pool.wait_ge(s["m1"], u1)
                    g.tensor_tensor(mrest[:].unsqueeze(2), mmax[i][:].unsqueeze(2), mtok[i][:, :, 0:1], ALU.add
                                    ).then_inc(s["mrest"], 1)
                    pool.wait_ge(s["mrest"], u1)
                    g.tensor_tensor(mtok[i][:, :, 1:2], mrest[:].unsqueeze(2), minus_one[:].unsqueeze(2), ALU.mult).then_inc(s["m2"], 1)

                def block_pool(qt, last):
                    base = (b * QT + qt) * BU
                    for rel in range(LEAD, LEAD + BU):
                        if not (last and rel >= BU):
                            shift(base + rel, rel % 2)

                for rel in range(LEAD):
                    shift(b * UNITS + rel, rel % 2)
                with pool.Fori(0, QT - 1) as qt:
                    block_pool(qt, False)
                block_pool(QT - 1, True)

        @block.scalar
        def _(act):
            a = nc.scalar
            act.wait_ge(s["tern_ps"], 1)
            a.activation(tern_t[:], bk_(0, 0).rearrange("p (c n) -> p c n", c=C), ACT.Copy).then_inc(s["tern"], 1)
            act.wait_ge(s["const"], CONSTS)
            act.wait_ge(s["eps_rows"], 1)
            with act.Fori(0, B) as b:
                def copy_x(n):
                    for j in range(W):
                        act.wait_ge(s["xnT_ps"], n[j])
                        a.activation(xnT[j][:], bk_(j, 1)[:, 0:D].rearrange("p (c q) -> p c q", c=C), ACT.Copy
                                     ).then_inc(s["xnT"], 1)

                def phi(n):
                    for j in range(W):
                        act.wait_ge(s["q_ps"], n[j])
                        a.activation(phiqT[j][:], bk_(j, 1)[:, 0:D].rearrange("p (c q) -> p c q", c=C), ACT.Relu, scale=-1.0
                                     ).then_inc(s["negq"], 1)
                        act.wait_ge(s["kv_ps"], n[j])
                        a.activation(phik[j][:], bk_(j, 2)[:, 0:D].rearrange("p (c q) -> p c q", c=C), ACT.Relu, scale=-1.0
                                     ).then_inc(s["negk"], 1)
                        act.wait_ge(s["negq"], n[j])
                        a.activation(phiqT[j][:], phiqT[j][:], ACT.Exp, scale=-1.0).then_inc(s["expq"], 1)
                        act.wait_ge(s["negk"], n[j])
                        a.activation(phik[j][:], phik[j][:], ACT.Exp, scale=-1.0).then_inc(s["expk"], 1)
                        a.activation(vaug[j][:, :, 0:HD], bk_(j, 2)[:, D:2 * D].rearrange("p (h d) -> p h d", d=HD), ACT.Copy
                                     ).then_inc(s["vaug"], 1)

                def rest_act(p, more):
                    n = tile_numbers(act, b, p)
                    for j in range(W):
                        act.wait_ge(s["phikT_ps"], n[j])
                        a.activation(phikT[j], bk_(j, 1)[:, 0:D].rearrange("p (c q) -> p c q", c=C), ACT.Copy
                                     ).then_inc(s["phikT"], 1)
                    for j in range(W):
                        act.wait_ge(s["ot_ps"], n[j])
                        act.wait_ge(s["state"], n[j] + (b + 1))
                        a.activation(osb[j][:], bk_(j, 1), ACT.Identity, bias=eps_rows[:]).then_inc(s["osb"], 1)
                    for j in range(W):
                        act.wait_ge(s["onT_ps"], n[j])
                        a.activation(on0T[j], bk_(j, 1)[:, 0:D].rearrange("p (c q) -> p c q", c=C), ACT.Copy
                                     ).then_inc(s["onT"], 1)
                    for j in range(W):
                        act.wait_ge(s["xn2T_ps"], n[j])
                        a.activation(xn2T[j][:], bk_(j, 1)[:, 0:D].rearrange("p (c q) -> p c q", c=C), ACT.Copy
                                     ).then_inc(s["xn2T"], 1)
                    if more:
                        following = tile_numbers(act, b, p + 1)
                        copy_x(following)
                    for j in range(W):
                        act.wait_ge(s["u_ps"], n[j])
                        a.activation(eu[j], bk_(j, 3), ACT.Tanh, scale=0.5).then_inc(s["tu"], 1)
                    for j in range(W):
                        act.wait_ge(s["part0"], n[j])
                        a.activation(qtok[j][:, :, 0:3, :],
                                     part[j][0][:, 0:D].rearrange("p (h d) -> p h d", d=HD).unsqueeze(2).broadcast_to([P, H, 3, HD]),
                                     ACT.Copy)
                        act.wait_ge(s["part2"], n[j])
                        a.activation(qtok[j][:, :, 5, :], part[j][2][:, 0:D].rearrange("p (h d) -> p h d", d=HD), ACT.Copy
                                     ).then_inc(s["qtok_a"], 1)
                    for j in range(W):
                        act.wait_ge(s["dv"], n[j])
                        a.activation(gt[j][:, 1:2], gt[j][:, 0:1], ACT.Exp).then_inc(s["edv"], 1)
                    if more:
                        phi(following)
                    for j in range(W):
                        act.wait_ge(s["sT_ps"], n[j])
                        a.activation(sT[j], bk_(j, 3).rearrange("p (c q) -> p c q", q=P), ACT.Copy).then_inc(s["sT"], 1)

                n0 = tile_numbers(act, b, 0)
                copy_x(n0)
                phi(n0)
                with act.Fori(0, PAIRS - 1) as p:
                    rest_act(p, True)
                rest_act(PAIRS - 1, False)

                def shift_rows(unit, g, h, qt):
                    act.wait_ge(s["mT_ps"], unit + (1 + UNIT_RING))
                    a.activation(qaug[MROW:P, G * g + h, bass.ds(qt * QB, QB)],
                                 bank[MISC_BANK][MROW:P, 0:QB // 2].bitcast(BF16), ACT.Copy).then_inc(s["mT"], 1)

                def turn(blk, half):
                    act.wait_ge(s["turn_ps"], blk * 2 + (half + 1))
                    a.activation(on1T[:, 2 * half:2 * half + 2, :, :],
                                 bank[MISC_BANK][:].rearrange("p (r c q) -> p r c q", r=2, c=C), ACT.Copy).then_inc(s["turn"], 1)

                def block_act(qt, first_block, last_block):
                    blk = act.snap(b * QT + qt)
                    ubase = act.snap(blk * BU)
                    for g in range(KV):
                        grp = act.snap(blk * KV + g)
                        first = act.snap(grp * SUBS)
                        chunk0 = act.snap(grp * KC)
                        for kc in range(KC):
                            act.wait_ge(s["av"], chunk0 + (kc + 1))
                            for h in range(G):
                                i = G * kc + h
                                act.wait_ge(s["s_ps"], first + (i + 1))
                                a.activation(probs[i % (2 * G)], bank[S_BANK[i % S_RING]][:], ACT.Exp, scale=HD ** -0.5
                                             ).then_inc(s["probs"], 1)
                            rel = G * g + G + kc // 4
                            if kc in SHIFT_AT and not (last_block and rel >= BU):
                                shift_rows(ubase + rel, *unit_at(rel, qt))
                            if kc in TURN_AT and g == 0 and not first_block:
                                turn(blk - 1, TURN_AT.index(kc))
                        act.wait_ge(s["av"], chunk0 + (KC + PROBS_RING))
                        if g > 0 or not first_block:
                            act.wait_ge(s["out_ps"], grp)
                        a.activation(osb1, bank[O_BANK][:], ACT.Copy).then_inc(s["osb1"], 1)

                for rel in range(LEAD - 1):
                    shift_rows(b * UNITS + rel, *unit_at(rel, 0))
                block_act(0, True, False)
                with act.Fori(1, QT - 1) as qt:
                    block_act(qt, False, False)
                block_act(QT - 1, False, True)
                for half in range(2):
                    turn(b * QT + (QT - 1), half)

        @block.vector
        def _(dve):
            v = nc.vector
            raw = am[0][:, 0:C * D]
            mag = am[1][:, 0:C * D]
            a_gt = am[0][:, C * D:2 * C * D]
            tern = am[1][:, C * D:2 * C * D]
            dve.wait_ge(s["w_small"], 32)
            v.scalar_tensor_tensor(out=mag, in0=raw, scalar=-1.0, in1=raw, op0=ALU.mult, op1=ALU.max).then_inc(s["abs_set"], 1)
            dve.wait_ge(s["abs_set"], 1)
            v.reduce_sum(tsum[:], mag, AX_X).then_inc(s["sum_set"], 1)
            dve.wait_ge(s["total_ps"], 1)
            v.tensor_scalar(delta[:, 0:1], bk_(0, 1)[:, 0:1], 1.0 / (D * D), 0.7, ALU.mult, ALU.mult).then_inc(s["delta_set"], 1)
            dve.wait_ge(s["delta_set"], 1)
            v.tensor_scalar(delta[:, 1:2], delta[:, 0:1], -1.0, None, ALU.mult).then_inc(s["ndelta"], 1)
            v.tensor_scalar(a_gt, raw, delta[:, 0:1], None, ALU.is_gt).then_inc(s["above"], 1)
            dve.wait_ge(s["ndelta"], 1)
            dve.wait_ge(s["above"], 1)
            v.scalar_tensor_tensor(out=tern, in0=raw, scalar=delta[:, 1:2], in1=a_gt, op0=ALU.is_lt, op1=ALU.subtract,
                                   reverse1=True).then_inc(s["above"], 1)
            dve.wait_ge(s["above"], 2)
            v.tensor_scalar(tern, tern, alpha_col[:], None, ALU.mult).then_inc(s["above"], 1)
            v.memset(kaug[MROW:P, :, :], 0.0).then_inc(s["k_rows"], 1)
            dve.wait_ge(s["k_rows"], 1)
            v.memset(kaug[MROW:MROW + 2, :, :], 1.0).then_inc(s["k_rows"], 1)
            dve.wait_ge(s["const"], CONSTS)
            v.reduce_sum(eps_rows[:], eps_pick[:], AX_X).then_inc(s["eps_rows"], 1)
            v.memset(spare[:, 0:1], 0.0).then_inc(s["xb"], W)
            v.memset(spare[:, 12:13], 0.0).then_inc(s["kt"], W)
            v.memset(spare[:, 13:14], 0.0).then_inc(s["qb"], W)
            v.memset(spare[:, 1:2], 0.0).then_inc(s["probs"], S_RING)
            v.memset(spare[:, 2:3], 0.0).then_inc(s["av"], PROBS_RING)
            v.memset(spare[:, 3:4], 0.0).then_inc(s["mx"], MX_RING)
            v.memset(spare[:, 4:5], 0.0).then_inc(s["m2"], UNIT_RING)
            v.memset(spare[:, 5:6], 0.0).then_inc(s["mT_ps"], UNIT_RING)
            v.memset(spare[:, 8:9], 0.0).then_inc(s["mT"], 1)
            v.memset(spare[:, 9:10], 0.0).then_inc(s["osb1"], 1)
            v.memset(spare[:, 10:11], 0.0).then_inc(s["on1"], 1)
            v.memset(spare[:, 11:12], 0.0).then_inc(s["y"], 1)
            for j in range(W):
                v.memset(spare[:, 6 + j:7 + j], 0.0).then_inc(s_st_out[j], 16)
            dve.wait_ge(s["w_all"], 16 * LOADS)

            with dve.Fori(0, B) as b:
                def statistics_x(j, n):
                    dve.wait_ge(s_x_in[j], (n[0] + (W - 1)) * (16 // W))
                    v.bn_stats(st6[j][:], xin[j][:]).then_inc(s["st"], 1)
                    dve.wait_ge(s["st"], n[j])
                    v.memset(carry_v[:], 0.0)
                    v.bn_aggr(mv[j][:], st6[j][:]).then_inc(s["mv"], 1)

                def normalized(src, ready, done, j, n):
                    dve.wait_ge(s[ready], n[j])
                    v.tensor_scalar(xn[j][:], src[j][:], mv[j][:, 0:1], rstd[j][:], ALU.subtract, ALU.mult
                                    ).then_inc(s[done], 1)

                def phi(n):
                    for j in range(W):
                        dve.wait_ge(s["expq"], n[j])
                        v.scalar_tensor_tensor(out=phiqT[j][:].rearrange("p c q -> p (c q)"), in0=bk_(j, 1)[:, 0:D], scalar=1.0,
                                               in1=phiqT[j][:].rearrange("p c q -> p (c q)"), op0=ALU.add, op1=ALU.max
                                               ).then_inc(s["phiq"], 1)
                        dve.wait_ge(s["expk"], n[j])
                        dve.wait_ge(s["vaug"], n[j])
                        v.scalar_tensor_tensor(out=phik[j][:].rearrange("p c q -> p (c q)"), in0=bk_(j, 2)[:, 0:D], scalar=1.0,
                                               in1=phik[j][:].rearrange("p c q -> p (c q)"), op0=ALU.add, op1=ALU.max
                                               ).then_inc(s["phik"], 1)

                def rest_dve(p, more):
                    n = tile_numbers(dve, b, p)
                    tok = [dve.snap(p * (W * P) + j * P) for j in range(W)]

                    for j in range(W):
                        dve.wait_ge(s["u0_ps"], n[j])
                        v.tensor_tensor(osb[j][:].rearrange("p (c h e) -> p c h e", c=C, h=8),
                                        bk_(j, 3).rearrange("p (c h e) -> p c h e", c=C, h=8),
                                        head_rows[:].unsqueeze(1).unsqueeze(3).broadcast_to([P, C, 8, HB]),
                                        ALU.mult).then_inc(s["um"], 1)
                    for half in range(C):
                        for j in range(W):
                            for q in (2 * half, 2 * half + 1):
                                dve.wait_ge(s["at_ps"], (n[0] - 1) * 4 + (half * 2 * W + 2 * j + q % 2 + 1))
                                v.tensor_tensor(am3[j][:, 4 * q:4 * q + 4, :],
                                                bk_(j, (1, 2, 0, 3)[q]).rearrange("p (h q) -> p h q", h=4),
                                                causal[:].unsqueeze(1).broadcast_to([P, 4, P]), ALU.mult).then_inc(s["am"], 1)
                    for j in range(W):
                        dve.wait_ge(s["den_ps"], n[j])
                        o = bk_(j, 2).rearrange("p (h e) -> p h e", e=HB)
                        v.reciprocal(rden[j][:].unsqueeze(2), o[:, :, HD:HD + 1]).then_inc(s["rden"], 1)
                        dve.wait_ge(s["rden"], n[j])
                        v.tensor_tensor(on0[j], bk_(j, 2).rearrange("p (h e) -> p h e", e=HB)[:, :, 0:HD],
                                        rden[j][:].unsqueeze(2).broadcast_to([P, H, HD]), ALU.mult).then_inc(s["on"], 1)
                    for j in range(W):
                        dve.wait_ge(s["y0_ps"], n[j])
                        dve.wait_ge(s["xb"], n[j] + W)
                        v.tensor_tensor(x1[j][:], x1[j][:], bk_(j, 0)[:, 0:D], ALU.add).then_inc(s["x1"], 1)
                        dve.wait_ge(s["x1"], n[j])
                        v.bn_stats(st6[j][:], x1[j][:]).then_inc(s["st2"], 1)
                        dve.wait_ge(s["st2"], n[j])
                        v.memset(carry_v[:], 0.0)
                        v.bn_aggr(mv[j][:], st6[j][:]).then_inc(s["mv2"], 1)
                        normalized(x1, "rstd2", "xn2", j, n)
                    if more:
                        following = tile_numbers(dve, b, p + 1)
                        for j in range(W):
                            statistics_x(j, following)
                        for j in range(W):
                            dve.wait_ge(s["xn2T_ps"], n[j])
                            normalized(xin, "rstd", "xn", j, following)
                    for j in range(W):
                        dve.wait_ge(s["prj_ps"], n[j])
                        v.tensor_tensor(qkv[j][:], bk_(j, 2)[:, 0:QKV1 + E], bias1_row[:], ALU.add).then_inc(s["qkv"], 1)
                    for j in range(W):
                        dve.wait_ge(s["qkv"], n[j])
                        v.tensor_copy(part[j][0], qkv[j][:, 0:NQK]).then_inc(s["part0"], 1)
                    for j in range(W):
                        v.max(out=top8[j][:], in_=qkv[j][:, QKV1:QKV1 + E]).then_inc(s["topv"], 1)
                    for j in range(W):
                        dve.wait_ge(s["topv"], n[j])
                        dve.wait_ge(s["part0"], n[j])
                        v.tensor_tensor(qkv[j][:, 0:NQK], qkv[j][:, 0:NQK], part[j][0], ALU.subtract).then_inc(s["rest"], 1)
                    for j in range(W):
                        v.max_index(out=top8i[j][:], in_max=top8[j][:], in_values=qkv[j][:, QKV1:QKV1 + E]).then_inc(s["topi"], 1)
                    for j in range(W):
                        dve.wait_ge(s["rest"], n[j])
                        v.tensor_copy(part[j][1], qkv[j][:, 0:NQK]).then_inc(s["part1"], 1)
                    for j in range(W):
                        v.tensor_tensor(gt[j][:, 0:1], top8[j][:, 1:2], top8[j][:, 0:1], ALU.subtract).then_inc(s["dv"], 1)
                    for j in range(W):
                        dve.wait_ge(s["part1"], n[j])
                        v.tensor_tensor(part[j][2], qkv[j][:, 0:NQK], part[j][1], ALU.subtract).then_inc(s["part2"], 1)
                    for j in range(W):
                        dve.wait_ge(s["topi"], n[j])
                        v.tensor_copy(top8f[j][:], top8i[j][:]).then_inc(s["topf"], 1)
                    for j in range(W):
                        dve.wait_ge(s["tu"], n[j])
                        v.scalar_tensor_tensor(out=su[j], in0=eu[j], scalar=1.0, in1=bk_(j, 3), op0=ALU.add, op1=ALU.mult
                                               ).then_inc(s["su"], 1)
                    for j in range(W):
                        dve.wait_ge(s["edv"], n[j])
                        v.tensor_scalar(gt[j][:, 2:3], gt[j][:, 1:2], 1.0, 2.0, ALU.add, ALU.mult).then_inc(s["gsum"], 1)
                    for j in range(W):
                        dve.wait_ge(s["gsum"], n[j])
                        v.reciprocal(gt[j][:, 3:4], gt[j][:, 2:3]).then_inc(s["w1st"], 1)
                    for j in range(W):
                        dve.wait_ge(s["w1st"], n[j])
                        v.tensor_tensor(gt[j][:, 4:5], gt[j][:, 3:4], gt[j][:, 1:2], ALU.mult).then_inc(s["w2nd"], 1)
                    for j in range(W):
                        dve.wait_ge(s["topf"], n[j])
                        v.tensor_scalar(g1[j][:], expert_no[:], top8f[j][:, 0:1], gt[j][:, 3:4], ALU.is_equal, ALU.mult
                                        ).then_inc(s["g1"], 1)
                    for j in range(W):
                        dve.wait_ge(s["w2nd"], n[j])
                        v.tensor_scalar(g2[j][:], expert_no[:], top8f[j][:, 1:2], gt[j][:, 4:5], ALU.is_equal, ALU.mult
                                        ).then_inc(s["g2"], 1)
                    for j in range(W):
                        dve.wait_ge(s["g1"], n[j])
                        dve.wait_ge(s["g2"], n[j])
                        v.tensor_tensor(g1[j][:], g1[j][:], g2[j][:], ALU.add).then_inc(s["gw"], 1)
                    if more:
                        phi(following)
                    for j in range(W):
                        dve.wait_ge(s["ve_ps"], n[j])
                        dve.wait_ge(s["su"], n[j])
                        v.tensor_tensor(su[j], su[j], bk_(j, 0), ALU.mult).then_inc(s["sv"], 1)
                    for j in range(W):
                        dve.wait_ge(s["qa_ps"], n[j])
                        v.tensor_copy(qaug[0:ROWS, 0:8, bass.ds(tok[j], P)],
                                      bk_(j, 1).bitcast(BF16).rearrange("p (h q) -> p h q", h=8)[0:ROWS]).then_inc(s["qa"], 1)
                        dve.wait_ge(s["qb_ps"], n[j])
                        v.tensor_copy(qaug[0:ROWS, 8:16, bass.ds(tok[j], P)],
                                      bk_(j, 2).bitcast(BF16).rearrange("p (h q) -> p h q", h=8)[0:ROWS]).then_inc(s["qb"], 1)
                    for j in range(W):
                        dve.wait_ge(s["kt_ps"], n[j])
                        v.tensor_copy(kaug[0:ROWS, :, bass.ds(tok[j], P)],
                                      bk_(j, 1).bitcast(BF16)[0:ROWS, 0:KV * P].rearrange("p (h q) -> p h q", h=KV)
                                      ).then_inc(s["kt"], 1)
                    for j in range(W):
                        dve.wait_ge(s["y1_ps"], n[j])
                        dve.wait_ge(s["x1b"], n[j])
                        v.tensor_tensor(xres[:, bass.ds(p * W + j, 1), :], x1[j][:].unsqueeze(1),
                                        bk_(j, 0)[:, 0:D].unsqueeze(1), ALU.add).then_inc(s["xres"], 1)

                n0 = tile_numbers(dve, b, 0)
                for j in range(W):
                    dve.wait_ge(s_st_out[j], (b * (TILES // W) + 1) * 16)
                    statistics_x(j, n0)
                for j in range(W):
                    normalized(xin, "rstd", "xn", j, n0)
                phi(n0)
                with dve.Fori(0, PAIRS - 1) as p:
                    rest_dve(p, True)
                rest_dve(PAIRS - 1, False)

                def maxima(first, i, k):
                    dve.wait_ge(s["mx_ps"], first + (k + 1))
                    v.reduce_max(mx[i][:, k // 4, k % 4:k % 4 + 1], bank[MX_BANK[k % MX_RING]][:], AX_X).then_inc(s["mx"], 1)

                def unit_maximum(unit, first, i):
                    dve.wait_ge(s["mx"], first + (16 + MX_RING))
                    dve.wait_ge(s["m2"], unit + 1)
                    v.reduce_max(mmax[i][:], mx[i][:], AX_X).then_inc(s["mmax"], 1)

                def normalize(grp, g):
                    o = bank[MISC_BANK][:].rearrange("p (r h e) -> p r h e", r=RB, h=G)
                    dve.wait_ge(s["out_ps"], grp + 1)
                    v.reciprocal(rden1[:].unsqueeze(3), o[:, :, :, HD:HD + 1]).then_inc(s["rden1"], 1)
                    dve.wait_ge(s["rden1"], grp + 1)
                    v.tensor_tensor(on1.rearrange("p r (h g d) -> p r h g d", h=G, g=KV)[:, :, :, g, :], o[:, :, :, 0:HD],
                                    rden1[:].unsqueeze(3).broadcast_to([P, RB, G, HD]), ALU.mult).then_inc(s["on1"], 1)

                def projected(qt, r):
                    dve.wait_ge(s["y_ps"], b * TILES + qt * RB + (r + 1))
                    dve.wait_ge(s_st_out[r % W], (b * (TILES // W) + qt * (RB // W) + (r // W + 1)) * 16)
                    v.tensor_tensor(ytile[r % W][:].unsqueeze(1), xres[:, bass.ds(qt * RB + r, 1), :],
                                    bank[MISC_BANK][:, 0:D].unsqueeze(1), ALU.add).then_inc(s["y"], 1)

                def block_dve(qt, first_block, last_block):
                    base = dve.snap((b * QT + qt) * BU)
                    grp = dve.snap((b * QT + qt) * KV)
                    for g in range(KV):
                        for kc in range(KC):
                            rel = G * g + LEAD + kc // 4
                            if not (last_block and rel >= BU):
                                if kc % 4 == 0:
                                    first = dve.snap((base + rel) * 16)
                                for k in range(4 * (kc % 4), 4 * (kc % 4) + 4):
                                    maxima(first, rel % 2, k)
                                if kc % 4 == 3:
                                    unit_maximum(base + rel, first, rel % 2)
                            if kc == OUT_AT and (g > 0 or not first_block):
                                normalize(grp + (g - 1), (g - 1) % KV)
                            if kc in PROJ_AT and g == 0 and not first_block:
                                projected(qt - 1, PROJ_AT.index(kc))

                for rel in range(LEAD):
                    first = dve.snap((b * UNITS + rel) * 16)
                    for kk in range(16):
                        maxima(first, rel % 2, kk)
                    unit_maximum(b * UNITS + rel, first, rel % 2)
                block_dve(0, True, False)
                with dve.Fori(1, QT - 1) as qt:
                    block_dve(qt, False, False)
                block_dve(QT - 1, False, True)
                normalize((b + 1) * (QT * KV) - 1, KV - 1)
                for r in range(RB):
                    projected(QT - 1, r)

        @block.tensor
        def _(pe):
            t = nc.tensor
            mm = t.matmul
            pe.wait_ge(s["const"], CONSTS)
            pe.wait_ge(s["sum_set"], 1)
            mm(bk_(0, 1)[:, 0:1], ones[:], tsum[:], start=True, stop=True).then_inc(s["total_ps"], 1)
            pe.wait_ge(s["above"], 3)
            for c in range(C):
                for o in range(C):
                    last = t.transpose(bk_(0, 0)[:, c * D + o * P:c * D + (o + 1) * P],
                                       am[1][:, C * D + o * D + c * P:C * D + o * D + (c + 1) * P], ident[:])
            last.then_inc(s["tern_ps"], 1)
            pe.wait_ge(s["w_all"], 16 * LOADS)
            pe.wait_ge(s["tern"], 1)
            pe.wait_ge(s["k_rows"], 2)
            with pe.Fori(0, B) as b:
                def turn_x(n):
                    for j in range(W):
                        pe.wait_ge(s["xn"], n[j])
                        for c in range(C):
                            last = t.transpose(bk_(j, 1)[:, c * P:(c + 1) * P], xn[j][:, c * P:(c + 1) * P], ident[:])
                        last.then_inc(s["xnT_ps"], 1)

                def project_x(n, before):
                    for j in range(W):
                        pe.wait_ge(s["xnT"], n[j])
                        for m in range(C):
                            for c in range(C):
                                last = mm(bk_(j, 1)[:, m * P:(m + 1) * P], wqkv[:, c, m * P:(m + 1) * P], xnT[j][:, c, :],
                                          start=c == 0, stop=c == C - 1)
                        last.then_inc(s["q_ps"], 1)
                        if before is not None:
                            pe.wait_ge(s["qkv"], before[j])
                        for c in range(C):
                            last = mm(bk_(j, 2), xnT[j][:, c, :], wqkv[:, c, D:3 * D], start=c == 0, stop=c == C - 1)
                        last.then_inc(s["kv_ps"], 1)

                def rest_pe(p, more):
                    n = tile_numbers(pe, b, p)
                    for j in range(W):
                        pe.wait_ge(s["phik"], n[j])
                        pe.wait_ge(s["kt"], n[j])
                        for c in range(C):
                            last = t.transpose(bk_(j, 1)[:, c * P:(c + 1) * P], phik[j][:, c, :], ident[:])
                        last.then_inc(s["phikT_ps"], 1)
                        pe.wait_ge(s["vaug"], n[j])
                        for c in range(C):
                            last = mm(bk_(j, 3)[:, c * D:(c + 1) * D], phik[j][:, c, :],
                                      vaug[j][:, 8 * c:8 * c + 8, :].rearrange("p h e -> p (h e)"), start=True, stop=True)
                        last.then_inc(s["u0_ps"], 1)
                    for half in range(C):
                        for j in range(W):
                            pe.wait_ge(s["phikT"], n[j])
                            pe.wait_ge(s["phiqx"], (n[j] - (j + 1)) * 2 + (half * W + j + 1))
                            for q in (2 * half, 2 * half + 1):
                                if q == 1:
                                    pe.wait_ge(s["qb"], n[j])
                                if q == 2:
                                    pe.wait_ge(s["um"], n[j])
                                mm(bk_(j, (1, 2, 0, 3)[q]), phikT[j][:, half, :],
                                   phiqx[j][:, (q % 2) * 512:(q % 2 + 1) * 512], start=True, stop=True).then_inc(s["at_ps"], 1)
                    for j in range(W):
                        pe.wait_ge(s["am"], (n[0] - 1) * 4 + (2 * W + 2 * j + 2))
                        pe.wait_ge(s["state"], n[j] + b)
                        for g in range(KV):
                            mm(bk_(j, 1)[:, g * P:(g + 1) * P], state[j][:, g * P:(g + 1) * P], phiqT[j][:, g // 2, :],
                               start=g == 0, stop=False, skip_group_check=True)
                        for g in range(KV):
                            for h in range(G):
                                last = mm(bk_(j, 1)[HB * h:HB * (h + 1), g * P:(g + 1) * P], vaug[j][:, G * g + h, :],
                                          am3[j][:, G * g + h, :], start=False, stop=True, skip_group_check=True)
                        last.then_inc(s["ot_ps"], 1)
                    for j in range(W):
                        pe.wait_ge(s["osb"], n[j])
                        for g in range(KV):
                            last = t.transpose(bk_(j, 2)[:, g * P:(g + 1) * P], osb[j][:, g * P:(g + 1) * P], ident[:])
                        last.then_inc(s["den_ps"], 1)
                        for c in range(C):
                            mm(bk_(j, 0)[:, 0:D], xnT[j][:, c, :], tern_t[:, c, :], start=c == 0, stop=False)
                    for j in range(W):
                        pe.wait_ge(s["on"], n[j])
                        for c in range(C):
                            last = t.transpose(bk_(j, 1)[:, c * P:(c + 1) * P], am[j][:, c * P:(c + 1) * P], ident[:])
                        last.then_inc(s["onT_ps"], 1)
                    for j in range(W):
                        pe.wait_ge(s["onT"], n[j])
                        for c in range(C):
                            last = mm(bk_(j, 0)[:, 0:D], on0T[j][:, c, :], wout0[:, c, :], start=False, stop=c == C - 1)
                        last.then_inc(s["y0_ps"], 1)
                    for j in range(W):
                        pe.wait_ge(s["xn2"], n[j])
                        for c in range(C):
                            last = t.transpose(bk_(j, 1)[:, c * P:(c + 1) * P], xn[j][:, c * P:(c + 1) * P], ident[:])
                        last.then_inc(s["xn2T_ps"], 1)
                    for j in range(W):
                        pe.wait_ge(s["xn2T"], n[j])
                        for c in range(C):
                            last = mm(bk_(j, 2)[:, 0:QKV1 + E], xn2T[j][:, c, :], w1[:, c, :], start=c == 0, stop=c == C - 1)
                        last.then_inc(s["prj_ps"], 1)
                    if more:
                        following = tile_numbers(pe, b, p + 1)
                        turn_x(following)
                    for j in range(W):
                        for c in range(C):
                            last = mm(bk_(j, 3), xn2T[j][:, c, :], wu[:, c, :], start=c == 0, stop=c == C - 1)
                        last.then_inc(s["u_ps"], 1)
                    if more:
                        project_x(following, n)
                    for j in range(W):
                        for c in range(C):
                            last = mm(bk_(j, 0), xn2T[j][:, c, :], wve[:, c, :], start=c == 0, stop=c == C - 1)
                        last.then_inc(s["ve_ps"], 1)

                    def to_rows(j, bank_, tok, heads):
                        dst = bk_(j, bank_).bitcast(BF16)
                        for i, h in enumerate(heads):
                            last = t.transpose(dst[0:ROWS, i * P:(i + 1) * P], tok[j][:, h, 0:PARTS, :].rearrange("p s d -> p (s d)"),
                                               ident_b[:])
                        return last

                    for j in range(W):
                        pe.wait_ge(s["qtok_a"], n[j])
                        pe.wait_ge(s["qtok_p"], n[j] * 2)
                        if more:
                            pe.wait_ge(s["phiq"], following[j])
                            pe.wait_ge(s["phik"], following[j])
                        to_rows(j, 1, qtok, range(0, 8)).then_inc(s["qa_ps"], 1)
                        pe.wait_ge(s["part0"], n[j])
                        to_rows(j, 2, qtok, range(8, 16)).then_inc(s["qb_ps"], 1)
                    for j in range(W):
                        pe.wait_ge(s["ktok"], n[j])
                        pe.wait_ge(s["qa"], n[j])
                        to_rows(j, 1, ktok, range(KV)).then_inc(s["kt_ps"], 1)
                    for j in range(W):
                        pe.wait_ge(s["sg"], n[j])
                        for c in range(ER // P):
                            last = t.transpose(bk_(j, 3)[:, c * P:(c + 1) * P], su[j][:, c * P:(c + 1) * P], ident[:])
                        last.then_inc(s["sT_ps"], 1)
                    for j in range(W):
                        pe.wait_ge(s["sT"], n[j])
                        for c in range(ER // P):
                            last = mm(bk_(j, 0)[:, 0:D], sT[j][:, c, :], woe[:, c, :], start=c == 0, stop=c == ER // P - 1)
                        last.then_inc(s["y1_ps"], 1)

                n0 = tile_numbers(pe, b, 0)
                turn_x(n0)
                project_x(n0, None)
                with pe.Fori(0, PAIRS - 1) as p:
                    rest_pe(p, True)
                rest_pe(PAIRS - 1, False)

                def maxima(first, gg, h, qt, k):
                    pe.wait_ge(s["mx"], first + (k + 1))
                    mm(bank[MX_BANK[k % MX_RING]][:], qaug[0:ROWS, G * gg + h, bass.ds(qt * QB + (k // 4) * P, P)],
                       kaug[0:ROWS, gg, (k % 4) * 512:(k % 4 + 1) * 512], start=True, stop=True).then_inc(s["mx_ps"], 1)

                def shift_rows(unit, i):
                    pe.wait_ge(s["m2"], unit + (1 + UNIT_RING))
                    pe.wait_ge(s["mT"], unit + 1)
                    for r in range(RB):
                        last = t.transpose(bank[MISC_BANK][MROW:P, r * (P // 2):(r + 1) * (P // 2)].bitcast(BF16), mtok[i][:, r, :],
                                           ident_b[:])
                    last.then_inc(s["mT_ps"], 1)

                def to_queries(grp):
                    pe.wait_ge(s["osb1"], grp + 2)
                    pe.wait_ge(s["on1"], grp + 1)
                    for r in range(RB):
                        last = t.transpose(bank[MISC_BANK][:, r * P:(r + 1) * P], osb1[:, r * P:(r + 1) * P], ident[:])
                    last.then_inc(s["out_ps"], 1)

                def turn(blk, half, units):
                    pe.wait_ge(s["on1"], (blk + 1) * KV + 1)
                    if half == 0:
                        pe.wait_ge(s["mT"], units + 1)
                    else:
                        pe.wait_ge(s["turn"], blk * 2 + 1)
                    for r in range(2):
                        for c in range(C):
                            last = t.transpose(bank[MISC_BANK][:, (C * r + c) * P:(C * r + c + 1) * P],
                                               on1[:, 2 * half + r, c * P:(c + 1) * P], ident[:])
                    last.then_inc(s["turn_ps"], 1)

                def project(blk, r, units):
                    pe.wait_ge(s["turn"], blk * 2 + 2)
                    pe.wait_ge(s["y"], blk * RB + (r + 1))
                    pe.wait_ge(s["mT"], units + 1)
                    for c in range(C):
                        last = mm(bank[MISC_BANK][:, 0:D], on1T[:, r, c, :], wout1[:, c, :], start=c == 0, stop=c == C - 1)
                    last.then_inc(s["y_ps"], 1)

                def block_pe(qt, first_block, last_block):
                    blk = pe.snap(b * QT + qt)
                    base = pe.snap(blk * BU)
                    grp0 = pe.snap(blk * KV)

                    def weighted(first, g, kc):
                        pe.wait_ge(s["probs"], first + (G * (kc + 1) + S_RING))
                        for h in range(G):
                            last = mm(bank[O_BANK][HB * h:HB * (h + 1), :], v1[:, kc, g, :], probs[(G * kc + h) % (2 * G)],
                                      start=kc == 0, stop=kc == KC - 1, skip_group_check=True)
                        last.then_inc(s["av"], 1)

                    for g in range(KV):
                        first = pe.snap((grp0 + g) * SUBS)
                        for kc in range(KC):
                            rel = G * g + LEAD + kc // 4
                            if kc % 4 == 0 and not (last_block and rel >= BU):
                                mfirst = pe.snap((base + rel) * 16)
                            for h in range(G):
                                i = G * kc + h
                                if kc == 0:
                                    pe.wait_ge(s["mT"], base + (G * g + h + 2))
                                pe.wait_ge(s["probs"], first + (i + 1))
                                mm(bank[S_BANK[i % S_RING]][:], kaug[:, g, kc * P:(kc + 1) * P],
                                   qaug[:, G * g + h, bass.ds(qt * QB, QB)], start=True, stop=True).then_inc(s["s_ps"], 1)
                                if not (last_block and rel >= BU):
                                    for k in MAXIMA_AFTER[h]:
                                        maxima(mfirst, *unit_at(rel, qt), 4 * (kc % 4) + k)
                                if h == AV_AFTER and kc >= 1:
                                    if kc == 1:
                                        pe.wait_ge(s["osb1"], grp0 + (g + 1))
                                    weighted(first, g, kc - 1)
                            if kc == OUT_AT and (g > 0 or not first_block):
                                to_queries(grp0 + (g - 1))
                            if kc in TURN_AT and g == 0 and not first_block:
                                turn(blk - 1, TURN_AT.index(kc), base + (G + 1))
                            if kc in PROJ_AT and g == 0 and not first_block:
                                project(blk - 1, PROJ_AT.index(kc), base + (G + 2 if kc < 10 else G + 3))
                            rel = G * g + G + kc // 4
                            if kc in SHIFT_AT and not (last_block and rel >= BU):
                                if kc == 2:
                                    pe.wait_ge(s["on1"], grp0 + (g + 1))
                                if kc == 6 and g == 0 and not first_block:
                                    pe.wait_ge(s["turn"], blk * 2)
                                if kc == 10 and g == 0 and not first_block:
                                    pe.wait_ge(s["y"], blk * RB)
                                if kc == 14 and g == 0 and not first_block:
                                    pe.wait_ge(s["y"], blk * RB + 1)
                                shift_rows(base + rel, rel % 2)
                        weighted(first, g, KC - 1)

                pe.wait_ge(s["xres"], (b + 1) * TILES)
                pe.wait_ge(s["v1"], (b + 1) * TILES)
                for rel in range(LEAD):
                    first = pe.snap((b * UNITS + rel) * 16)
                    for k in range(16):
                        maxima(first, *unit_at(rel, 0), k)
                    if rel >= 1:
                        shift_rows(b * UNITS + (rel - 1), (rel - 1) % 2)
                block_pe(0, True, False)
                with pe.Fori(1, QT - 1) as qt:
                    block_pe(qt, False, False)
                block_pe(QT - 1, False, True)
                to_queries((b + 1) * (QT * KV) - 1)
                for half in range(2):
                    turn(b * QT + (QT - 1), half, (b + 1) * UNITS)
                for r in range(RB):
                    project(b * QT + (QT - 1), r, (b + 1) * UNITS)

    return nc


_INS = ["L0_attn_x", "L0_attn_W_qkv", "L0_attn_W_out", "L0_ffn_weight", "L0_ffn_alpha", "L0_ffn_bias",
        "L1_attn_Wq", "L1_attn_bq", "L1_attn_Wk", "L1_attn_bk", "L1_attn_Wv", "L1_attn_bv", "L1_attn_Wo", "L1_attn_bo",
        "L1_ffn_gate_w", "L1_ffn_Wu", "L1_ffn_Wv", "L1_ffn_Wo"]


def kernel(**inputs):
    import numpy as _np
    import concourse.bacc as _bacc
    from concourse import mybir as _mybir
    from concourse.bass_utils import run_bass_kernel_spmd as _run

    nc = _bacc.Bacc("TRN2", target_bir_lowering=False, num_devices=1)
    arrays, args = {}, []
    for name in _INS:
        a = _np.ascontiguousarray(inputs[name])
        arrays[f"in_{name}_dram"] = a
        args.append(nc.dram_tensor(f"in_{name}_dram", a.shape, _mybir.dt.from_np(a.dtype), kind="ExternalInput").ap())
    args.append(nc.dram_tensor("out_0_dram", (B, S, D), _mybir.dt.float32, kind="ExternalOutput").ap())
    two_layers(nc, *args)
    r = _run(nc, [arrays], core_ids=[0])
    return r.results[0]["out_0_dram"]
```

```python
from contextlib import ExitStack

import concourse.bass as bass
from concourse import mybir

F32 = mybir.dt.float32
BF16 = mybir.dt.bfloat16
U32 = mybir.dt.uint32
ALU = mybir.AluOpType
ACT = mybir.ActivationFunctionType
AX_X = mybir.AxisListType.X

P = 128
B, S, D = 4, 2048, 256
H, HD = 16, 16
KV = 4
G = H // KV
E, R = 8, 64
ER = E * R
C = D // P
TILES = S // P
W = 2
PAIRS = TILES // W
QB = 512
QT = S // QB
RB = QB // P
KC = S // P
UNITS = QT * KV * G
SUBS = KC * G
PARTS = 6
ROWS = PARTS * HD
MROW = ROWS
HB = 32
QKV1 = D + 2 * KV * HD
EPS_LN = 1e-5
EPS_DEN = 1e-6
LOADS = 17
CONSTS = 9


def two_layers(nc, x, W_qkv, W_out, W_tern, alpha, bias0, Wq, bq, Wk, bk, Wv, bv, Wo, bo, gate_w, Wu, Wve, Woe, out):
    ctx = ExitStack()
    with ctx:
        def sb(name, shape, dt=F32):
            return ctx.enter_context(nc.sbuf_tensor(name, shape, dt))

        def sem(name):
            return ctx.enter_context(nc.semaphore(name))

        bank = [ctx.enter_context(nc.psum_tensor(f"bank{i}", [P, 512], F32)) for i in range(8)]

        wqkv = sb("wqkv", [P, C, 3 * D])
        wout0 = sb("wout0", [P, C, D])
        tern_t = sb("tern_t", [P, C, D])
        w1 = sb("w1", [P, C, QKV1 + E])
        wu = sb("wu", [P, C, ER])
        wve = sb("wve", [P, C, ER])
        wout1 = sb("wout1", [P, C, D])
        woe = sb("woe", [P, ER // P, D])
        bias0_row = sb("bias0_row", [P, D])
        bo_row = sb("bo_row", [P, D])
        bias1_row = sb("bias1_row", [P, QKV1 + E])
        minus_half = sb("minus_half", [P, 1])
        minus_one = sb("minus_one", [P, RB])
        eps_ln = sb("eps_ln", [P, 1])
        carry = sb("carry", [P, W])
        carry_v = sb("carry_v", [P, 1])
        spare = sb("spare", [P, 15])
        eps_rows = sb("eps_rows", [P, 1])
        alpha_col = sb("alpha_col", [P, 1])
        ones = sb("ones", [P, P])
        tsum = sb("tsum", [P, 1])
        delta = sb("delta", [P, 2])
        ident = sb("ident", [P, P])
        ident_b = sb("ident_b", [P, P], BF16)
        causal = sb("causal", [P, P])
        head_rows = sb("head_rows", [P, 8])
        eps_pick = sb("eps_pick", [P, G])
        expert_no = sb("expert_no", [P, E])

        qaug = sb("qaug", [P, H, S], BF16)
        kaug = sb("kaug", [P, KV, S], BF16)
        v1 = sb("v1", [P, KC, KV, HB])
        xres = sb("xres", [P, TILES, D])

        def per_tile(name, shape, dt=F32):
            return [sb(f"{name}{j}", shape, dt) for j in range(W)]

        xin = per_tile("xin", [P, D])
        x1 = per_tile("x1", [P, D])
        st6 = per_tile("st6", [P, 6])
        mv = per_tile("mv", [P, 2])
        rstd = per_tile("rstd", [P, 1])
        xn = per_tile("xn", [P, D])
        xnT = per_tile("xnT", [P, C, P])
        phiqT = per_tile("phiqT", [P, C, P])
        phik = per_tile("phik", [P, C, P])
        phiqx = per_tile("phiqx", [P, 8 * P])
        am = per_tile("am", [P, H * P])
        vaug = per_tile("vaug", [P, H, HB])
        state = [sb(f"state{j}", [P, C * 8 * HB]) for j in range(W)]
        osb = per_tile("osb", [P, KV * P])
        xn2T = per_tile("xn2T", [P, C, P])
        qkv = per_tile("qkv", [P, QKV1 + E])
        top8 = per_tile("top8", [P, 8])
        top8i = per_tile("top8i", [P, 8], U32)
        top8f = per_tile("top8f", [P, 8])
        gt = per_tile("gt", [P, 8])
        rden = per_tile("rden", [P, H])
        g1 = per_tile("g1", [P, E])
        g2 = per_tile("g2", [P, E])
        phikT = [xn[j][:].rearrange("p (c q) -> p c q", c=C) for j in range(W)]
        phiqx3 = [phiqx[j][:].rearrange("p (h q) -> p h q", h=8) for j in range(W)]
        am3 = [am[j][:].rearrange("p (h q) -> p h q", h=H) for j in range(W)]
        eu = [am[j][:, 0:ER] for j in range(W)]
        on0 = [am[j][:, 0:D].rearrange("p (h d) -> p h d", d=HD) for j in range(W)]
        on0T = [osb[j][:, 0:D].rearrange("p (c q) -> p c q", c=C) for j in range(W)]
        su = [am[j][:, ER:2 * ER] for j in range(W)]
        sT = [am[j][:, 2 * ER:3 * ER].rearrange("p (c q) -> p c q", q=P) for j in range(W)]
        NQK = D + KV * HD
        part = [[am[j][:].bitcast(BF16)[:, 6 * ER + i * NQK:6 * ER + (i + 1) * NQK] for i in range(3)] for j in range(W)]
        qtok = [phiqx[j][:].bitcast(BF16)[:, 0:H * ROWS].rearrange("p (h s d) -> p h s d", h=H, d=HD) for j in range(W)]
        ktok = [phiqx[j][:].bitcast(BF16)[:, H * ROWS:(H + KV) * ROWS].rearrange("p (h s d) -> p h s d", h=KV, d=HD)
                for j in range(W)]

        probs = [(phiqx[0], phiqx[1], am[1])[min(i // 2, 2)][:, (i % 2 if i < 4 else i - 4) * QB:(i % 2 + 1 if i < 4 else i - 3) * QB]
                 for i in range(2 * G)]
        on1 = am[0][:, 0:RB * D].rearrange("p (r n) -> p r n", r=RB)
        on1T = am[0][:, RB * D:2 * RB * D].rearrange("p (r c q) -> p r c q", r=RB, c=C)
        osb1 = osb[0][:]
        rden1 = sb("rden_1", [P, RB, G])
        ytile = xn
        mx = [sb(f"mx{i}", [P, RB, 4]) for i in range(2)]
        mmax = [sb(f"mmax{i}", [P, RB]) for i in range(2)]
        mrest = sb("mrest", [P, RB])
        mtok = [sb(f"mtok{i}", [P, RB, HB], BF16) for i in range(2)]

        names = """w_small w_all filled const total_ps abs_set sum_set delta_set ndelta above tern tern_ps k_rows eps_rows
        xb st mv veps veps2 rstd xn xnT_ps xnT q_ps kv_ps negq negk expq expk vaug phiq phik phikT_ps phikT
        phiqx phiqx_a u0_ps um state at_ps am ot_ps osb den_ps rden on onT_ps onT y0_ps x1 st2 mv2 rstd2 xn2 xn2T_ps xn2T prj_ps u_ps ve_ps
        qkv part0 rest part1 part2 qtok_a qtok_v ktok v1 qa_ps qb_ps qa qb kt_ps kt topv topi topf dv edv gsum w1st w2nd
        g1 g2 gw tu su sv x1b sg_v sg_p sT_ps sT y1_ps xres
        mx_ps mx mmax m1 mrest m2 mT_ps mT s_ps probs av osb1 out_ps rden1 on1 turn_ps turn y_ps y""".split()
        s = {n: sem("s_" + n) for n in names}
        s_x_in = [sem(f"s_x_in{j}") for j in range(W)]
        s_st_out = [sem(f"s_st_out{j}") for j in range(W)]

        def bk_(j, i):
            return bank[4 * j + i][:]

        AT_BANK = (1, 0, 2, 3)
        S_BANK, MX_BANK, O_BANK, MISC_BANK = (0, 1), (2, 3, 4, 5), 6, 7

        AV_AFTER, MAXIMA_AFTER = 1, ((0,), (), (), (1, 2, 3))
        OUT_AT, TURN_AT, PROJ_AT, SHIFT_AT = 1, (3, 4), (7, 8, 9, 11), (2, 6, 10, 14)

        PROBS_RING, S_RING, MX_RING, UNIT_RING = 2, 2, 4, 2
        LEAD = G + 1
        BU = KV * G

        WIDE_FROM = (BU - LEAD) * 16 // G * G
        WIDE_RING = 4

        def score_bank(last_block, i):
            if last_block and i >= WIDE_FROM:
                return (S_BANK + MX_BANK[:2])[i % WIDE_RING], WIDE_RING if i >= WIDE_FROM + WIDE_RING else S_RING
            return S_BANK[i % S_RING], S_RING

        def unit_at(rel, qt):
            return (rel // G) % KV, rel % G, qt + rel // BU

        def tile_numbers(eng, b, p):
            return [eng.snap(b * TILES + p * W + (j + 1)) for j in range(W)]


        block = ctx.enter_context(nc.Block())
        x_flat = x.rearrange("b s d -> (b s) d")
        out_flat = out.rearrange("b s d -> (b s) d")

        @block.sync
        def _(sp):
            for dst, src in ((am[0][:, 0:C * D].rearrange("p (c n) -> p c n", c=C), W_tern.rearrange("(c p) n -> p c n", p=P)),
                             (alpha_col[:], alpha.partition_broadcast(P))):
                sp.dma_start(dst, src).then_inc(s["w_small"], 16)
            loads = [(wqkv[:], W_qkv.rearrange("(c p) n -> p c n", p=P)), (bias0_row[:], bias0.partition_broadcast(P)),
                     (bo_row[:], bo.partition_broadcast(P)), (wout0[:], W_out.rearrange("(c p) n -> p c n", p=P)),
                     (wout1[:], Wo.rearrange("(c p) n -> p c n", p=P))]
            at = 0
            for w, n in ((Wq, D), (Wk, KV * HD), (Wv, KV * HD), (gate_w, E)):
                loads.append((w1[:, :, at:at + n], w.rearrange("(c p) n -> p c n", p=P)))
                at += n
            at = 0
            for w, n in ((bq, D), (bk, KV * HD), (bv, KV * HD)):
                loads.append((bias1_row[:, at:at + n], w.partition_broadcast(P)))
                at += n
            for c in range(C):
                for w, dst in ((Wu, wu), (Wve, wve)):
                    loads.append((dst[:, c, :].rearrange("p (e r) -> p e r", e=E),
                                  w[:, c * P:(c + 1) * P, :].rearrange("e p r -> p e r")))
            loads.append((woe[:], Woe.rearrange("e r n -> (e r) n").rearrange("(c p) n -> p c n", p=P)))
            for dst, src in loads:
                sp.dma_start(dst, src).then_inc(s["w_all"], 16)
            assert len(loads) == LOADS
            def load_pair(b, p):
                n = tile_numbers(sp, b, p)
                for j in range(W):
                    sp.wait_ge(s["xb"], n[j])
                    sp.dma_start(xin[j][:], x_flat[bass.ds((n[j] - 1) * P, P), :]).then_inc(s_x_in[j], 16)

            def sequence(b, more):
                with sp.Fori(1, PAIRS) as p:
                    load_pair(b, p)
                if more:
                    load_pair(b + 1, 0)
                with sp.Fori(0, QT) as qt:
                    for r in range(RB):
                        n = sp.snap(b * TILES + qt * RB + (r + 1))
                        sp.wait_ge(s["y"], n + 1)
                        sp.dma_start(out_flat[bass.ds((n - 1) * P, P), :], ytile[r % W][:]).then_inc(s_st_out[r % W], 16)
            for j in range(W):
                sp.dma_start(xin[j][:], x_flat[j * P:(j + 1) * P, :]).then_inc(s_x_in[j], 16)
            with sp.Fori(0, B - 1) as b:
                sequence(b, True)
            sequence(B - 1, False)
            for j in range(W):
                sp.wait_ge(s_st_out[j], 16 * (B * TILES // W + 1))

        @block.gpsimd
        def _(pool):
            g = nc.gpsimd
            g.memset(bias1_row[:, QKV1:QKV1 + E], 0.0).then_inc(s["filled"], 1)
            g.memset(minus_half[:], -0.5).then_inc(s["filled"], 1)
            g.memset(minus_one[:], -1.0).then_inc(s["filled"], 1)
            g.memset(eps_ln[:], EPS_LN).then_inc(s["filled"], 1)
            g.memset(ones[:], 1.0).then_inc(s["filled"], 1)
            g.memset(ident[:], 0.0).then_inc(s["filled"], 1)
            g.memset(ident_b[:], 0.0).then_inc(s["filled"], 1)
            g.memset(causal[:], 1.0).then_inc(s["filled"], 1)
            g.memset(head_rows[:], 1.0).then_inc(s["filled"], 1)
            g.memset(eps_pick[:], 0.0).then_inc(s["filled"], 1)
            for j in range(W):
                g.memset(vaug[j][:], 0.0).then_inc(s["filled"], 1)
            g.memset(v1[:], 0.0).then_inc(s["filled"], 1)
            for i in range(2):
                g.memset(mtok[i][:], 0.0).then_inc(s["filled"], 1)
            g.iota(expert_no[:], pattern=[[1, E]], base=0, channel_multiplier=0,
                   allow_small_or_imprecise_dtypes=True).then_inc(s["filled"], 1)
            pool.wait_ge(s["filled"], 16)
            for t in (ident, ident_b):
                g.affine_select(out=t[:], in_=t[:], compare_op=ALU.not_equal, fill=1.0, base=0,
                                pattern=[[-1, P]], channel_multiplier=1).then_inc(s["const"], 1)
            g.affine_select(out=causal[:], in_=causal[:], compare_op=ALU.is_ge, fill=0.0, base=0,
                            pattern=[[1, P]], channel_multiplier=-1).then_inc(s["const"], 1)
            g.affine_select(out=head_rows[:], in_=head_rows[:], compare_op=ALU.is_ge, fill=0.0, base=0,
                            pattern=[[-HD, 8]], channel_multiplier=1).then_inc(s["const"], 1)
            g.affine_select(out=eps_pick[:], in_=eps_pick[:], compare_op=ALU.not_equal, fill=EPS_DEN, base=-HD,
                            pattern=[[-HB, G]], channel_multiplier=1).then_inc(s["const"], 1)
            for j in range(W):
                g.memset(vaug[j][:, :, HD:HD + 1], 1.0).then_inc(s["const"], 1)
            g.memset(v1[:, :, :, HD:HD + 1], 1.0).then_inc(s["const"], 1)
            pool.wait_ge(s["const"], 8)
            g.affine_select(out=head_rows[:], in_=head_rows[:], compare_op=ALU.is_ge, fill=0.0, base=HD - 1,
                            pattern=[[HD, 8]], channel_multiplier=-1).then_inc(s["const"], 1)
            pool.wait_ge(s["const"], CONSTS)
            pool.wait_ge(s["w_all"], 16 * LOADS)
            with pool.Fori(0, B) as b:
                g.memset(state[0][:], 0.0).then_inc(s["state"], 1)
                def front_pool(n):
                    for j in range(W):
                        pool.wait_ge(s["mv"], n[j])
                        g.tensor_tensor(rstd[j][:], mv[j][:, 1:2], eps_ln[:], ALU.add).then_inc(s["veps"], 1)
                    for j in range(W):
                        pool.wait_ge(s["veps"], n[j])
                        g.tensor_tensor(rstd[j][:], rstd[j][:], minus_half[:], ALU.pow).then_inc(s["rstd"], 1)

                def rest_pool(p, more):
                    n = tile_numbers(pool, b, p)
                    tile0 = pool.snap(p * W)
                    for half in range(C):
                        if half == 1:
                            for j in range(W):
                                pool.wait_ge(s["xres"], n[j])
                                g.tensor_tensor(x1[j][:], xin[j][:], bias0_row[:], ALU.add).then_inc(s["xb"], 1)
                        for j in range(W):
                            if half == 0:
                                pool.wait_ge(s["phiq"], n[j])
                                pool.wait_ge(s["kt"], n[j])
                            else:
                                pool.wait_ge(s["at_ps"], (n[0] - 1) * 4 + (2 * j + 2))
                            heads = 8 if half == 0 else 4
                            g.tensor_tensor(phiqx3[j][:, 0:heads, :],
                                            phiqT[j][:, half, :].unsqueeze(1).broadcast_to([P, heads, P]),
                                            head_rows[:, 0:heads].unsqueeze(2).broadcast_to([P, heads, P]), ALU.mult
                                            ).then_inc(s["phiqx"], 1)
                    pool.wait_ge(s["um"], n[0])
                    g.tensor_tensor(state[1][:], state[0][:], osb[0][:], ALU.add).then_inc(s["state"], 1)
                    if more:
                        front_pool(tile_numbers(pool, b, p + 1))
                    pool.wait_ge(s["state"], n[0] + (b + 1))
                    pool.wait_ge(s["um"], n[1])
                    pool.wait_ge(s["ot_ps"], n[0])
                    g.tensor_tensor(state[0][:], state[1][:], osb[1][:], ALU.add).then_inc(s["state"], 1)
                    for j in range(W):
                        pool.wait_ge(s["mv2"], n[j])
                        g.tensor_tensor(rstd[j][:], mv[j][:, 1:2], eps_ln[:], ALU.add).then_inc(s["veps2"], 1)
                        pool.wait_ge(s["veps2"], n[j])
                        g.tensor_tensor(rstd[j][:], rstd[j][:], minus_half[:], ALU.pow).then_inc(s["rstd2"], 1)
                    for j in range(W):
                        pool.wait_ge(s["xn2"], n[j])
                        g.tensor_tensor(x1[j][:], x1[j][:], bo_row[:], ALU.add).then_inc(s["x1b"], 1)
                    for j in range(W):
                        pool.wait_ge(s["qkv"], n[j])
                        g.tensor_tensor(v1[:, bass.ds(tile0 + j, 1), :, 0:HD],
                                        qkv[j][:, NQK:QKV1].rearrange("p (a h d) -> p a h d", a=1, d=HD),
                                        ones[:, 0:KV * HD].rearrange("p (a h d) -> p a h d", a=1, d=HD), ALU.mult
                                        ).then_inc(s["v1"], 1)
                    for j in range(W):
                        pool.wait_ge(s["part2"], n[j])
                        g.tensor_tensor(carry[:, j:j + 1], minus_half[:], minus_half[:], ALU.mult)
                        k = [part[j][i][:, D:NQK].rearrange("p (h d) -> p h d", d=HD) for i in range(3)]
                        for slots, i in ((slice(0, 4, 3), 0), (slice(5, 6), 0), (slice(1, 5, 3), 1), (slice(2, 3), 2)):
                            src = k[i].unsqueeze(2)
                            if slots.step:
                                src = src.broadcast_to([P, KV, 2, HD])
                            last = g.tensor_scalar(ktok[j][:, :, slots, :], src, 1.0, None, ALU.mult)
                        last.then_inc(s["ktok"], 1)
                    for j in range(1, W):
                        pool.wait_ge(s["su"], n[j])
                        pool.wait_ge(s["gw"], n[j])
                        silu = su[j].rearrange("p (e r) -> p e r", e=E)
                        g.tensor_tensor(silu, silu, g1[j][:].unsqueeze(2).broadcast_to([P, E, R]), ALU.mult).then_inc(s["sg_p"], W)

                front_pool(tile_numbers(pool, b, 0))
                with pool.Fori(0, PAIRS - 1) as p:
                    rest_pool(p, True)
                rest_pool(PAIRS - 1, False)

                def shift(unit, i):
                    u1 = pool.snap(unit + 1)
                    pool.wait_ge(s["mmax"], u1)
                    pool.wait_ge(s["mT_ps"], u1)
                    g.tensor_tensor(mtok[i][:, :, 0:1], mmax[i][:].unsqueeze(2), minus_one[:].unsqueeze(2), ALU.mult).then_inc(s["m1"], 1)
                    pool.wait_ge(s["m1"], u1)
                    g.tensor_tensor(mrest[:].unsqueeze(2), mmax[i][:].unsqueeze(2), mtok[i][:, :, 0:1], ALU.add
                                    ).then_inc(s["mrest"], 1)
                    pool.wait_ge(s["mrest"], u1)
                    g.tensor_tensor(mtok[i][:, :, 1:2], mrest[:].unsqueeze(2), minus_one[:].unsqueeze(2), ALU.mult).then_inc(s["m2"], 1)

                def block_pool(qt, last):
                    base = (b * QT + qt) * BU
                    for rel in range(LEAD, LEAD + BU):
                        if not (last and rel >= BU):
                            shift(base + rel, rel % 2)

                for rel in range(LEAD):
                    shift(b * UNITS + rel, rel % 2)
                with pool.Fori(0, QT - 1) as qt:
                    block_pool(qt, False)
                block_pool(QT - 1, True)

        @block.scalar
        def _(act):
            a = nc.scalar
            act.wait_ge(s["tern_ps"], 1)
            a.activation(tern_t[:], bk_(0, 0).rearrange("p (c n) -> p c n", c=C), ACT.Copy).then_inc(s["tern"], 1)
            act.wait_ge(s["const"], CONSTS)
            act.wait_ge(s["eps_rows"], 1)
            with act.Fori(0, B) as b:
                def copy_x(n, tiles):
                    for j in tiles:
                        act.wait_ge(s["xnT_ps"], n[j])
                        a.activation(xnT[j][:], bk_(j, 3)[:, 0:D].rearrange("p (c q) -> p c q", c=C), ACT.Copy
                                     ).then_inc(s["xnT"], 1)

                def phi(n, j):
                    act.wait_ge(s["q_ps"], n[j])
                    a.activation(phiqT[j][:], bk_(j, 3)[:, 0:D].rearrange("p (c q) -> p c q", c=C), ACT.Relu, scale=-1.0
                                 ).then_inc(s["negq"], 1)
                    act.wait_ge(s["kv_ps"], n[j])
                    a.activation(phik[j][:], bk_(j, 2)[:, 0:D].rearrange("p (c q) -> p c q", c=C), ACT.Relu, scale=-1.0
                                 ).then_inc(s["negk"], 1)
                    act.wait_ge(s["negq"], n[j])
                    a.activation(phiqT[j][:], phiqT[j][:], ACT.Exp, scale=-1.0).then_inc(s["expq"], 1)
                    act.wait_ge(s["negk"], n[j])
                    a.activation(phik[j][:], phik[j][:], ACT.Exp, scale=-1.0).then_inc(s["expk"], 1)
                    a.activation(vaug[j][:, :, 0:HD], bk_(j, 2)[:, D:2 * D].rearrange("p (h d) -> p h d", d=HD), ACT.Copy
                                 ).then_inc(s["vaug"], 1)

                def rest_act(p, more):
                    n = tile_numbers(act, b, p)
                    for j in range(W):
                        act.wait_ge(s["phikT_ps"], n[j])
                        a.activation(phikT[j], bk_(j, 1)[:, 0:D].rearrange("p (c q) -> p c q", c=C), ACT.Copy
                                     ).then_inc(s["phikT"], 1)
                    for j in range(W):
                        act.wait_ge(s["at_ps"], (n[0] - 1) * 4 + (2 * j + 2))
                        for h in range(4, 8):
                            last = a.activation(phiqx3[j][:, h, :], phiqT[j][:, 1, :], ACT.Identity, scale=head_rows[:, h:h + 1])
                        last.then_inc(s["phiqx_a"], 1)
                    for j in range(W):
                        act.wait_ge(s["ot_ps"], n[j])
                        act.wait_ge(s["state"], n[j] + (b + 1))
                        a.activation(osb[j][:], bk_(j, 1), ACT.Identity, bias=eps_rows[:]).then_inc(s["osb"], 1)
                    if more:
                        following = tile_numbers(act, b, p + 1)
                        copy_x(following, (0,))
                    for j in range(W):
                        act.wait_ge(s["onT_ps"], n[j])
                        a.activation(on0T[j], bk_(j, 1)[:, 0:D].rearrange("p (c q) -> p c q", c=C), ACT.Copy
                                     ).then_inc(s["onT"], 1)
                    if more:
                        copy_x(following, (1,))
                        phi(following, 0)
                    for j in range(W):
                        act.wait_ge(s["xn2T_ps"], n[j])
                        a.activation(xn2T[j][:], bk_(j, 1)[:, 0:D].rearrange("p (c q) -> p c q", c=C), ACT.Copy
                                     ).then_inc(s["xn2T"], 1)
                    if more:
                        phi(following, 1)
                    for j in range(W):
                        act.wait_ge(s["u_ps"], n[j])
                        a.activation(eu[j], bk_(j, 1), ACT.Tanh, scale=0.5).then_inc(s["tu"], 1)
                        if j == 0:
                            for i in range(W):
                                act.wait_ge(s["dv"], n[i])
                                a.activation(gt[i][:, 1:2], gt[i][:, 0:1], ACT.Exp).then_inc(s["edv"], 1)
                    for j in range(W):
                        act.wait_ge(s["part0"], n[j])
                        a.activation(qtok[j][:, :, 0:3, :],
                                     part[j][0][:, 0:D].rearrange("p (h d) -> p h d", d=HD).unsqueeze(2).broadcast_to([P, H, 3, HD]),
                                     ACT.Copy)
                        act.wait_ge(s["part2"], n[j])
                        a.activation(qtok[j][:, :, 5, :], part[j][2][:, 0:D].rearrange("p (h d) -> p h d", d=HD), ACT.Copy
                                     ).then_inc(s["qtok_a"], 1)
                    for j in range(W):
                        act.wait_ge(s["sT_ps"], n[j])
                        a.activation(sT[j], bk_(j, 0).rearrange("p (c q) -> p c q", q=P), ACT.Copy).then_inc(s["sT"], 1)

                n0 = tile_numbers(act, b, 0)
                copy_x(n0, range(W))
                for j in range(W):
                    phi(n0, j)
                with act.Fori(0, PAIRS - 1) as p:
                    rest_act(p, True)
                rest_act(PAIRS - 1, False)

                def shift_rows(unit, g, h, qt):
                    act.wait_ge(s["mT_ps"], unit + (1 + UNIT_RING))
                    a.activation(qaug[MROW:P, G * g + h, bass.ds(qt * QB, QB)],
                                 bank[MISC_BANK][MROW:P, 0:QB // 2].bitcast(BF16), ACT.Copy).then_inc(s["mT"], 1)

                def turn(blk, half):
                    act.wait_ge(s["turn_ps"], blk * 2 + (half + 1))
                    a.activation(on1T[:, 2 * half:2 * half + 2, :, :],
                                 bank[MISC_BANK][:].rearrange("p (r c q) -> p r c q", r=2, c=C), ACT.Copy).then_inc(s["turn"], 1)

                def block_act(qt, first_block, last_block):
                    blk = act.snap(b * QT + qt)
                    ubase = act.snap(blk * BU)
                    for g in range(KV):
                        grp = act.snap(blk * KV + g)
                        first = act.snap(grp * SUBS)
                        chunk0 = act.snap(grp * KC)
                        for kc in range(KC):
                            act.wait_ge(s["av"], chunk0 + (kc + 1))
                            for h in range(G):
                                i = G * kc + h
                                act.wait_ge(s["s_ps"], first + (i + 1))
                                a.activation(probs[i % (2 * G)], bank[score_bank(last_block, g * SUBS + i)[0]][:], ACT.Exp, scale=HD ** -0.5
                                             ).then_inc(s["probs"], 1)
                            rel = G * g + G + kc // 4
                            if kc in SHIFT_AT and not (last_block and rel >= BU):
                                shift_rows(ubase + rel, *unit_at(rel, qt))
                            if kc in TURN_AT and g == 0 and not first_block:
                                turn(blk - 1, TURN_AT.index(kc))
                        act.wait_ge(s["av"], chunk0 + (KC + PROBS_RING))
                        if g > 0 or not first_block:
                            act.wait_ge(s["out_ps"], grp)
                        a.activation(osb1, bank[O_BANK][:], ACT.Copy).then_inc(s["osb1"], 1)

                for rel in range(LEAD - 1):
                    shift_rows(b * UNITS + rel, *unit_at(rel, 0))
                block_act(0, True, False)
                with act.Fori(1, QT - 1) as qt:
                    block_act(qt, False, False)
                block_act(QT - 1, False, True)
                for half in range(2):
                    turn(b * QT + (QT - 1), half)

        @block.vector
        def _(dve):
            v = nc.vector
            raw = am[0][:, 0:C * D]
            mag = am[1][:, 0:C * D]
            a_gt = am[0][:, C * D:2 * C * D]
            tern = am[1][:, C * D:2 * C * D]
            dve.wait_ge(s["w_small"], 32)
            v.scalar_tensor_tensor(out=mag, in0=raw, scalar=-1.0, in1=raw, op0=ALU.mult, op1=ALU.max).then_inc(s["abs_set"], 1)
            dve.wait_ge(s["abs_set"], 1)
            v.reduce_sum(tsum[:], mag, AX_X).then_inc(s["sum_set"], 1)
            dve.wait_ge(s["total_ps"], 1)
            v.tensor_scalar(delta[:, 0:1], bk_(0, 1)[:, 0:1], 1.0 / (D * D), 0.7, ALU.mult, ALU.mult).then_inc(s["delta_set"], 1)
            dve.wait_ge(s["delta_set"], 1)
            v.tensor_scalar(delta[:, 1:2], delta[:, 0:1], -1.0, None, ALU.mult).then_inc(s["ndelta"], 1)
            v.tensor_scalar(a_gt, raw, delta[:, 0:1], None, ALU.is_gt).then_inc(s["above"], 1)
            dve.wait_ge(s["ndelta"], 1)
            dve.wait_ge(s["above"], 1)
            v.scalar_tensor_tensor(out=tern, in0=raw, scalar=delta[:, 1:2], in1=a_gt, op0=ALU.is_lt, op1=ALU.subtract,
                                   reverse1=True).then_inc(s["above"], 1)
            dve.wait_ge(s["above"], 2)
            v.tensor_scalar(tern, tern, alpha_col[:], None, ALU.mult).then_inc(s["above"], 1)
            v.memset(kaug[MROW:P, :, :], 0.0).then_inc(s["k_rows"], 1)
            dve.wait_ge(s["k_rows"], 1)
            v.memset(kaug[MROW:MROW + 2, :, :], 1.0).then_inc(s["k_rows"], 1)
            dve.wait_ge(s["const"], CONSTS)
            v.reduce_sum(eps_rows[:], eps_pick[:], AX_X).then_inc(s["eps_rows"], 1)
            v.memset(spare[:, 0:1], 0.0).then_inc(s["xb"], W)
            v.memset(spare[:, 12:13], 0.0).then_inc(s["kt"], W)
            v.memset(spare[:, 13:14], 0.0).then_inc(s["qb"], W)
            v.memset(spare[:, 14:15], 0.0).then_inc(s["xres"], W)
            v.memset(spare[:, 1:2], 0.0).then_inc(s["probs"], S_RING)
            v.memset(spare[:, 2:3], 0.0).then_inc(s["av"], PROBS_RING)
            v.memset(spare[:, 3:4], 0.0).then_inc(s["mx"], MX_RING)
            v.memset(spare[:, 4:5], 0.0).then_inc(s["m2"], UNIT_RING)
            v.memset(spare[:, 5:6], 0.0).then_inc(s["mT_ps"], UNIT_RING)
            v.memset(spare[:, 8:9], 0.0).then_inc(s["mT"], 1)
            v.memset(spare[:, 9:10], 0.0).then_inc(s["osb1"], 1)
            v.memset(spare[:, 10:11], 0.0).then_inc(s["on1"], 1)
            v.memset(spare[:, 11:12], 0.0).then_inc(s["y"], 1)
            for j in range(W):
                v.memset(spare[:, 6 + j:7 + j], 0.0).then_inc(s_st_out[j], 16)
            dve.wait_ge(s["w_all"], 16 * LOADS)

            with dve.Fori(0, B) as b:
                def statistics_x(j, n):
                    dve.wait_ge(s_x_in[j], (n[0] + (W - 1)) * (16 // W))
                    v.bn_stats(st6[j][:], xin[j][:]).then_inc(s["st"], 1)
                    dve.wait_ge(s["st"], n[j])
                    v.memset(carry_v[:], 0.0)
                    v.bn_aggr(mv[j][:], st6[j][:]).then_inc(s["mv"], 1)

                def normalized(src, ready, done, j, n):
                    dve.wait_ge(s[ready], n[j])
                    v.tensor_scalar(xn[j][:], src[j][:], mv[j][:, 0:1], rstd[j][:], ALU.subtract, ALU.mult
                                    ).then_inc(s[done], 1)

                def phi(n):
                    for j in range(W):
                        dve.wait_ge(s["expq"], n[j])
                        v.scalar_tensor_tensor(out=phiqT[j][:].rearrange("p c q -> p (c q)"), in0=bk_(j, 3)[:, 0:D], scalar=1.0,
                                               in1=phiqT[j][:].rearrange("p c q -> p (c q)"), op0=ALU.add, op1=ALU.max
                                               ).then_inc(s["phiq"], 1)
                        dve.wait_ge(s["expk"], n[j])
                        dve.wait_ge(s["vaug"], n[j])
                        v.scalar_tensor_tensor(out=phik[j][:].rearrange("p c q -> p (c q)"), in0=bk_(j, 2)[:, 0:D], scalar=1.0,
                                               in1=phik[j][:].rearrange("p c q -> p (c q)"), op0=ALU.add, op1=ALU.max
                                               ).then_inc(s["phik"], 1)

                def rest_dve(p, more):
                    n = tile_numbers(dve, b, p)
                    tok = [dve.snap(p * (W * P) + j * P) for j in range(W)]

                    for j in range(W):
                        dve.wait_ge(s["u0_ps"], n[j])
                        v.tensor_tensor(osb[j][:].rearrange("p (c h e) -> p c h e", c=C, h=8),
                                        bk_(j, 3).rearrange("p (c h e) -> p c h e", c=C, h=8),
                                        head_rows[:].unsqueeze(1).unsqueeze(3).broadcast_to([P, C, 8, HB]),
                                        ALU.mult).then_inc(s["um"], 1)
                    for half in range(C):
                        for j in range(W):
                            for q in (2 * half, 2 * half + 1):
                                dve.wait_ge(s["at_ps"], (n[0] - 1) * 4 + (half * 2 * W + 2 * j + q % 2 + 1))
                                v.tensor_tensor(am3[j][:, 4 * q:4 * q + 4, :],
                                                bk_(j, AT_BANK[q]).rearrange("p (h q) -> p h q", h=4),
                                                causal[:].unsqueeze(1).broadcast_to([P, 4, P]), ALU.mult).then_inc(s["am"], 1)
                    if more:
                        following = tile_numbers(dve, b, p + 1)
                        for j in range(W):
                            statistics_x(j, following)
                        for j in range(W):
                            normalized(xin, "rstd", "xn", j, following)
                    for j in range(W):
                        dve.wait_ge(s["den_ps"], n[j])
                        o = bk_(j, 2).rearrange("p (h e) -> p h e", e=HB)
                        v.reciprocal(rden[j][:].unsqueeze(2), o[:, :, HD:HD + 1]).then_inc(s["rden"], 1)
                        dve.wait_ge(s["rden"], n[j])
                        v.tensor_tensor(on0[j], bk_(j, 2).rearrange("p (h e) -> p h e", e=HB)[:, :, 0:HD],
                                        rden[j][:].unsqueeze(2).broadcast_to([P, H, HD]), ALU.mult).then_inc(s["on"], 1)
                    for j in range(W):
                        dve.wait_ge(s["y0_ps"], n[j])
                        dve.wait_ge(s["xb"], n[j] + W)
                        v.tensor_tensor(x1[j][:], x1[j][:], bk_(j, 0)[:, 0:D], ALU.add).then_inc(s["x1"], 1)
                        dve.wait_ge(s["x1"], n[j])
                        v.bn_stats(st6[j][:], x1[j][:]).then_inc(s["st2"], 1)
                        dve.wait_ge(s["st2"], n[j])
                        v.memset(carry_v[:], 0.0)
                        v.bn_aggr(mv[j][:], st6[j][:]).then_inc(s["mv2"], 1)
                    for j in range(W):
                        normalized(x1, "rstd2", "xn2", j, n)
                    if more:
                        phi(following)
                    for j in range(W):
                        dve.wait_ge(s["prj_ps"], n[j])
                        v.tensor_tensor(qkv[j][:], bk_(j, 0)[:, 0:QKV1 + E], bias1_row[:], ALU.add).then_inc(s["qkv"], 1)
                    for j in range(W):
                        dve.wait_ge(s["qkv"], n[j])
                        v.tensor_copy(part[j][0], qkv[j][:, 0:NQK]).then_inc(s["part0"], 1)
                    for j in range(W):
                        v.max(out=top8[j][:], in_=qkv[j][:, QKV1:QKV1 + E]).then_inc(s["topv"], 1)
                    for j in range(W):
                        dve.wait_ge(s["topv"], n[j])
                        dve.wait_ge(s["part0"], n[j])
                        v.tensor_tensor(qkv[j][:, 0:NQK], qkv[j][:, 0:NQK], part[j][0], ALU.subtract).then_inc(s["rest"], 1)
                    for j in range(W):
                        v.max_index(out=top8i[j][:], in_max=top8[j][:], in_values=qkv[j][:, QKV1:QKV1 + E]).then_inc(s["topi"], 1)
                    for j in range(W):
                        dve.wait_ge(s["rest"], n[j])
                        v.tensor_copy(part[j][1], qkv[j][:, 0:NQK]).then_inc(s["part1"], 1)
                    for j in range(W):
                        v.tensor_tensor(gt[j][:, 0:1], top8[j][:, 1:2], top8[j][:, 0:1], ALU.subtract).then_inc(s["dv"], 1)
                    for j in range(W):
                        dve.wait_ge(s["part1"], n[j])
                        v.tensor_tensor(part[j][2], qkv[j][:, 0:NQK], part[j][1], ALU.subtract).then_inc(s["part2"], 1)
                    for j in range(W):
                        dve.wait_ge(s["topi"], n[j])
                        v.tensor_copy(top8f[j][:], top8i[j][:]).then_inc(s["topf"], 1)
                    def silu(j):
                        dve.wait_ge(s["tu"], n[j])
                        v.scalar_tensor_tensor(out=su[j], in0=eu[j], scalar=1.0, in1=bk_(j, 1), op0=ALU.add, op1=ALU.mult
                                               ).then_inc(s["su"], 1)

                    for j in range(W):
                        v.tensor_copy(qtok[j][:, :, 3:5, :], part[j][1][:, 0:D].rearrange("p (h d) -> p h d", d=HD)
                                      .unsqueeze(2).broadcast_to([P, H, 2, HD])).then_inc(s["qtok_v"], 1)
                    silu(0)
                    for j in range(W):
                        dve.wait_ge(s["edv"], n[j])
                        v.tensor_scalar(gt[j][:, 2:3], gt[j][:, 1:2], 1.0, 2.0, ALU.add, ALU.mult).then_inc(s["gsum"], 1)
                    for j in range(W):
                        dve.wait_ge(s["gsum"], n[j])
                        v.reciprocal(gt[j][:, 3:4], gt[j][:, 2:3]).then_inc(s["w1st"], 1)
                    for j in range(W):
                        dve.wait_ge(s["w1st"], n[j])
                        v.tensor_tensor(gt[j][:, 4:5], gt[j][:, 3:4], gt[j][:, 1:2], ALU.mult).then_inc(s["w2nd"], 1)
                    for j in range(W):
                        dve.wait_ge(s["topf"], n[j])
                        v.tensor_scalar(g1[j][:], expert_no[:], top8f[j][:, 0:1], gt[j][:, 3:4], ALU.is_equal, ALU.mult
                                        ).then_inc(s["g1"], 1)
                    for j in range(W):
                        dve.wait_ge(s["w2nd"], n[j])
                        v.tensor_scalar(g2[j][:], expert_no[:], top8f[j][:, 1:2], gt[j][:, 4:5], ALU.is_equal, ALU.mult
                                        ).then_inc(s["g2"], 1)
                    for j in range(W):
                        dve.wait_ge(s["g1"], n[j])
                        dve.wait_ge(s["g2"], n[j])
                        v.tensor_tensor(g1[j][:], g1[j][:], g2[j][:], ALU.add).then_inc(s["gw"], 1)
                    silu(1)

                    def rows(name, half, j):
                        dve.wait_ge(s[name + "_ps"], n[j])
                        v.tensor_copy(qaug[0:ROWS, 8 * half:8 * half + 8, bass.ds(tok[j], P)],
                                      bk_(j, 3 * half).bitcast(BF16).rearrange("p (h q) -> p h q", h=8)[0:ROWS]
                                      ).then_inc(s[name], 1)

                    dve.wait_ge(s["gw"], n[0])
                    dve.wait_ge(s["su"], n[0])
                    weighed = su[0].rearrange("p (e r) -> p e r", e=E)
                    v.tensor_tensor(weighed, weighed, g1[0][:].unsqueeze(2).broadcast_to([P, E, R]), ALU.mult
                                    ).then_inc(s["sg_v"], W)
                    for j in range(W):
                        dve.wait_ge(s["ve_ps"], n[j])
                        dve.wait_ge(s["sg_v" if j == 0 else "sg_p"], n[W - 1])
                        v.tensor_tensor(su[j], su[j], bk_(j, 2), ALU.mult).then_inc(s["sv"], 1)
                        rows("qa", 0, j)
                    for j in range(W):
                        rows("qb", 1, j)
                    for j in range(W):
                        dve.wait_ge(s["kt_ps"], n[j])
                        v.tensor_copy(kaug[0:ROWS, :, bass.ds(tok[j], P)],
                                      bk_(j, 1).bitcast(BF16)[0:ROWS, 0:KV * P].rearrange("p (h q) -> p h q", h=KV)
                                      ).then_inc(s["kt"], 1)
                    for j in range(W):
                        dve.wait_ge(s["y1_ps"], n[j])
                        dve.wait_ge(s["x1b"], n[j])
                        v.tensor_tensor(xres[:, bass.ds(p * W + j, 1), :], x1[j][:].unsqueeze(1),
                                        bk_(j, 2)[:, 0:D].unsqueeze(1), ALU.add).then_inc(s["xres"], 1)

                n0 = tile_numbers(dve, b, 0)
                for j in range(W):
                    dve.wait_ge(s_st_out[j], (b * (TILES // W) + 1) * 16)
                    statistics_x(j, n0)
                for j in range(W):
                    normalized(xin, "rstd", "xn", j, n0)
                phi(n0)
                with dve.Fori(0, PAIRS - 1) as p:
                    rest_dve(p, True)
                rest_dve(PAIRS - 1, False)

                def maxima(first, i, k):
                    dve.wait_ge(s["mx_ps"], first + (k + 1))
                    v.reduce_max(mx[i][:, k // 4, k % 4:k % 4 + 1], bank[MX_BANK[k % MX_RING]][:], AX_X).then_inc(s["mx"], 1)

                def unit_maximum(unit, first, i):
                    dve.wait_ge(s["mx"], first + (16 + MX_RING))
                    dve.wait_ge(s["m2"], unit + 1)
                    v.reduce_max(mmax[i][:], mx[i][:], AX_X).then_inc(s["mmax"], 1)

                def normalize(grp, g):
                    o = bank[MISC_BANK][:].rearrange("p (r h e) -> p r h e", r=RB, h=G)
                    dve.wait_ge(s["out_ps"], grp + 1)
                    v.reciprocal(rden1[:].unsqueeze(3), o[:, :, :, HD:HD + 1]).then_inc(s["rden1"], 1)
                    dve.wait_ge(s["rden1"], grp + 1)
                    v.tensor_tensor(on1.rearrange("p r (h g d) -> p r h g d", h=G, g=KV)[:, :, :, g, :], o[:, :, :, 0:HD],
                                    rden1[:].unsqueeze(3).broadcast_to([P, RB, G, HD]), ALU.mult).then_inc(s["on1"], 1)

                def projected(qt, r):
                    dve.wait_ge(s["y_ps"], b * TILES + qt * RB + (r + 1))
                    dve.wait_ge(s_st_out[r % W], (b * (TILES // W) + qt * (RB // W) + (r // W + 1)) * 16)
                    v.tensor_tensor(ytile[r % W][:].unsqueeze(1), xres[:, bass.ds(qt * RB + r, 1), :],
                                    bank[MISC_BANK][:, 0:D].unsqueeze(1), ALU.add).then_inc(s["y"], 1)

                def block_dve(qt, first_block, last_block):
                    base = dve.snap((b * QT + qt) * BU)
                    grp = dve.snap((b * QT + qt) * KV)
                    for g in range(KV):
                        for kc in range(KC):
                            rel = G * g + LEAD + kc // 4
                            if not (last_block and rel >= BU):
                                if kc % 4 == 0:
                                    first = dve.snap((base + rel) * 16)
                                for k in range(4 * (kc % 4), 4 * (kc % 4) + 4):
                                    maxima(first, rel % 2, k)
                                if kc % 4 == 3:
                                    unit_maximum(base + rel, first, rel % 2)
                            if kc == OUT_AT and (g > 0 or not first_block):
                                normalize(grp + (g - 1), (g - 1) % KV)
                            if kc in PROJ_AT and g == 0 and not first_block:
                                projected(qt - 1, PROJ_AT.index(kc))

                for rel in range(LEAD):
                    first = dve.snap((b * UNITS + rel) * 16)
                    for kk in range(16):
                        maxima(first, rel % 2, kk)
                    unit_maximum(b * UNITS + rel, first, rel % 2)
                block_dve(0, True, False)
                with dve.Fori(1, QT - 1) as qt:
                    block_dve(qt, False, False)
                block_dve(QT - 1, False, True)
                normalize((b + 1) * (QT * KV) - 1, KV - 1)
                for r in range(RB):
                    projected(QT - 1, r)

        @block.tensor
        def _(pe):
            t = nc.tensor
            mm = t.matmul
            pe.wait_ge(s["const"], CONSTS)
            pe.wait_ge(s["sum_set"], 1)
            mm(bk_(0, 1)[:, 0:1], ones[:], tsum[:], start=True, stop=True).then_inc(s["total_ps"], 1)
            pe.wait_ge(s["above"], 3)
            for c in range(C):
                for o in range(C):
                    last = t.transpose(bk_(0, 0)[:, c * D + o * P:c * D + (o + 1) * P],
                                       am[1][:, C * D + o * D + c * P:C * D + o * D + (c + 1) * P], ident[:])
            last.then_inc(s["tern_ps"], 1)
            pe.wait_ge(s["w_all"], 16 * LOADS)
            pe.wait_ge(s["tern"], 1)
            pe.wait_ge(s["k_rows"], 2)
            with pe.Fori(0, B) as b:
                def turn_x(n):
                    for j in range(W):
                        pe.wait_ge(s["xn"], n[j])
                        for c in range(C):
                            last = t.transpose(bk_(j, 3)[:, c * P:(c + 1) * P], xn[j][:, c * P:(c + 1) * P], ident[:])
                        last.then_inc(s["xnT_ps"], 1)

                def project_q(n, j):
                    pe.wait_ge(s["xnT"], n[j])
                    for m in range(C):
                        for c in range(C):
                            last = mm(bk_(j, 3)[:, m * P:(m + 1) * P], wqkv[:, c, m * P:(m + 1) * P], xnT[j][:, c, :],
                                      start=c == 0, stop=c == C - 1)
                    last.then_inc(s["q_ps"], 1)

                def project_kv(n, j):
                    for c in range(C):
                        last = mm(bk_(j, 2), xnT[j][:, c, :], wqkv[:, c, D:3 * D], start=c == 0, stop=c == C - 1)
                    last.then_inc(s["kv_ps"], 1)

                def rest_pe(p, more):
                    n = tile_numbers(pe, b, p)
                    for j in range(W):
                        pe.wait_ge(s["phik"], n[j])
                        pe.wait_ge(s["kt"], n[j])
                        for c in range(C):
                            last = t.transpose(bk_(j, 1)[:, c * P:(c + 1) * P], phik[j][:, c, :], ident[:])
                        last.then_inc(s["phikT_ps"], 1)
                        pe.wait_ge(s["vaug"], n[j])
                        pe.wait_ge(s["qb"], n[j])
                        for c in range(C):
                            last = mm(bk_(j, 3)[:, c * D:(c + 1) * D], phik[j][:, c, :],
                                      vaug[j][:, 8 * c:8 * c + 8, :].rearrange("p h e -> p (h e)"), start=True, stop=True)
                        last.then_inc(s["u0_ps"], 1)
                    for half in range(C):
                        for j in range(W):
                            pe.wait_ge(s["phikT"], n[j])
                            pe.wait_ge(s["phiqx"], (n[j] - (j + 1)) * 2 + (half * W + j + 1))
                            for q in (2 * half, 2 * half + 1):
                                if q == 3:
                                    pe.wait_ge(s["phiqx_a"], n[j])
                                if q == 2:
                                    pe.wait_ge(s["um"], n[j])
                                mm(bk_(j, AT_BANK[q]), phikT[j][:, half, :],
                                   phiqx[j][:, (q % 2) * 512:(q % 2 + 1) * 512], start=True, stop=True).then_inc(s["at_ps"], 1)
                    for j in range(W):
                        pe.wait_ge(s["am"], (n[0] - 1) * 4 + (2 * W + 2 * j + 2))
                        pe.wait_ge(s["state"], n[j] + b)
                        for g in range(KV):
                            mm(bk_(j, 1)[:, g * P:(g + 1) * P], state[j][:, g * P:(g + 1) * P], phiqT[j][:, g // 2, :],
                               start=g == 0, stop=False, skip_group_check=True)
                        for g in range(KV):
                            for h in range(G):
                                last = mm(bk_(j, 1)[HB * h:HB * (h + 1), g * P:(g + 1) * P], vaug[j][:, G * g + h, :],
                                          am3[j][:, G * g + h, :], start=False, stop=True, skip_group_check=True)
                        last.then_inc(s["ot_ps"], 1)
                    for j in range(W):
                        pe.wait_ge(s["osb"], n[j])
                        for g in range(KV):
                            last = t.transpose(bk_(j, 2)[:, g * P:(g + 1) * P], osb[j][:, g * P:(g + 1) * P], ident[:])
                        last.then_inc(s["den_ps"], 1)
                        for c in range(C):
                            mm(bk_(j, 0)[:, 0:D], xnT[j][:, c, :], tern_t[:, c, :], start=c == 0, stop=False)
                    if more:
                        following = tile_numbers(pe, b, p + 1)
                        turn_x(following)
                    for j in range(W):
                        pe.wait_ge(s["on"], n[j])
                        for c in range(C):
                            last = t.transpose(bk_(j, 1)[:, c * P:(c + 1) * P], am[j][:, c * P:(c + 1) * P], ident[:])
                        last.then_inc(s["onT_ps"], 1)
                    if more:
                        project_q(following, 0)
                    for j in range(W):
                        pe.wait_ge(s["onT"], n[j])
                        for c in range(C):
                            last = mm(bk_(j, 0)[:, 0:D], on0T[j][:, c, :], wout0[:, c, :], start=False, stop=c == C - 1)
                        last.then_inc(s["y0_ps"], 1)
                    if more:
                        project_kv(following, 0)
                        project_q(following, 1)
                    for j in range(W):
                        if j == 1 and more:
                            project_kv(following, 1)
                        pe.wait_ge(s["xn2"], n[j])
                        for c in range(C):
                            last = t.transpose(bk_(j, 1)[:, c * P:(c + 1) * P], xn[j][:, c * P:(c + 1) * P], ident[:])
                        last.then_inc(s["xn2T_ps"], 1)
                    for j in range(W):
                        pe.wait_ge(s["xn2T"], n[j])
                        for c in range(C):
                            last = mm(bk_(j, 0)[:, 0:QKV1 + E], xn2T[j][:, c, :], w1[:, c, :], start=c == 0, stop=c == C - 1)
                        last.then_inc(s["prj_ps"], 1)
                    for j in range(W):
                        for c in range(C):
                            last = mm(bk_(j, 1), xn2T[j][:, c, :], wu[:, c, :], start=c == 0, stop=c == C - 1)
                        last.then_inc(s["u_ps"], 1)
                    for j in range(W):
                        if more:
                            pe.wait_ge(s["phik"], following[j])
                        for c in range(C):
                            last = mm(bk_(j, 2), xn2T[j][:, c, :], wve[:, c, :], start=c == 0, stop=c == C - 1)
                        last.then_inc(s["ve_ps"], 1)

                    def to_rows(j, bank_, tok, heads):
                        dst = bk_(j, bank_).bitcast(BF16)
                        for i, h in enumerate(heads):
                            last = t.transpose(dst[0:ROWS, i * P:(i + 1) * P], tok[j][:, h, 0:PARTS, :].rearrange("p s d -> p (s d)"),
                                               ident_b[:])
                        return last

                    for j in range(W):
                        pe.wait_ge(s["qtok_a"], n[j])
                        pe.wait_ge(s["qtok_v"], n[j])
                        to_rows(j, 0, qtok, range(0, 8)).then_inc(s["qa_ps"], 1)
                    for j in range(W):
                        to_rows(j, 3, qtok, range(8, 16)).then_inc(s["qb_ps"], 1)
                    for j in range(W):
                        pe.wait_ge(s["ktok"], n[j])
                        pe.wait_ge(s["su"], n[j])
                        to_rows(j, 1, ktok, range(KV)).then_inc(s["kt_ps"], 1)
                    for j in range(W):
                        pe.wait_ge(s["sv"], n[j])
                        pe.wait_ge(s["qa"], n[j])
                        for c in range(ER // P):
                            last = t.transpose(bk_(j, 0)[:, c * P:(c + 1) * P], su[j][:, c * P:(c + 1) * P], ident[:])
                        last.then_inc(s["sT_ps"], 1)
                    for j in range(W):
                        pe.wait_ge(s["sT"], n[j])
                        for c in range(ER // P):
                            last = mm(bk_(j, 2)[:, 0:D], sT[j][:, c, :], woe[:, c, :], start=c == 0, stop=c == ER // P - 1)
                        last.then_inc(s["y1_ps"], 1)

                n0 = tile_numbers(pe, b, 0)
                turn_x(n0)
                for j in range(W):
                    project_q(n0, j)
                    project_kv(n0, j)
                with pe.Fori(0, PAIRS - 1) as p:
                    rest_pe(p, True)
                rest_pe(PAIRS - 1, False)

                def maxima(first, gg, h, qt, k):
                    pe.wait_ge(s["mx"], first + (k + 1))
                    mm(bank[MX_BANK[k % MX_RING]][:], qaug[0:ROWS, G * gg + h, bass.ds(qt * QB + (k // 4) * P, P)],
                       kaug[0:ROWS, gg, (k % 4) * 512:(k % 4 + 1) * 512], start=True, stop=True).then_inc(s["mx_ps"], 1)

                def shift_rows(unit, i):
                    pe.wait_ge(s["m2"], unit + (1 + UNIT_RING))
                    pe.wait_ge(s["mT"], unit + 1)
                    for r in range(RB):
                        last = t.transpose(bank[MISC_BANK][MROW:P, r * (P // 2):(r + 1) * (P // 2)].bitcast(BF16), mtok[i][:, r, :],
                                           ident_b[:])
                    last.then_inc(s["mT_ps"], 1)

                def to_queries(grp):
                    pe.wait_ge(s["osb1"], grp + 2)
                    pe.wait_ge(s["on1"], grp + 1)
                    for r in range(RB):
                        last = t.transpose(bank[MISC_BANK][:, r * P:(r + 1) * P], osb1[:, r * P:(r + 1) * P], ident[:])
                    last.then_inc(s["out_ps"], 1)

                def turn(blk, half, units):
                    pe.wait_ge(s["on1"], (blk + 1) * KV + 1)
                    if half == 0:
                        pe.wait_ge(s["mT"], units + 1)
                    else:
                        pe.wait_ge(s["turn"], blk * 2 + 1)
                    for r in range(2):
                        for c in range(C):
                            last = t.transpose(bank[MISC_BANK][:, (C * r + c) * P:(C * r + c + 1) * P],
                                               on1[:, 2 * half + r, c * P:(c + 1) * P], ident[:])
                    last.then_inc(s["turn_ps"], 1)

                def project(blk, r, units):
                    pe.wait_ge(s["turn"], blk * 2 + 2)
                    pe.wait_ge(s["y"], blk * RB + (r + 1))
                    pe.wait_ge(s["mT"], units + 1)
                    for c in range(C):
                        last = mm(bank[MISC_BANK][:, 0:D], on1T[:, r, c, :], wout1[:, c, :], start=c == 0, stop=c == C - 1)
                    last.then_inc(s["y_ps"], 1)

                def block_pe(qt, first_block, last_block):
                    blk = pe.snap(b * QT + qt)
                    base = pe.snap(blk * BU)
                    grp0 = pe.snap(blk * KV)

                    def weighted(first, g, kc):
                        pe.wait_ge(s["probs"], first + (G * (kc + 1) + S_RING))
                        for h in range(G):
                            last = mm(bank[O_BANK][HB * h:HB * (h + 1), :], v1[:, kc, g, :], probs[(G * kc + h) % (2 * G)],
                                      start=kc == 0, stop=kc == KC - 1, skip_group_check=True)
                        last.then_inc(s["av"], 1)

                    for g in range(KV):
                        first = pe.snap((grp0 + g) * SUBS)
                        for kc in range(KC):
                            rel = G * g + LEAD + kc // 4
                            if kc % 4 == 0 and not (last_block and rel >= BU):
                                mfirst = pe.snap((base + rel) * 16)
                            for h in range(G):
                                i = G * kc + h
                                if kc == 0:
                                    pe.wait_ge(s["mT"], base + (G * g + h + 2))
                                sbank, ring = score_bank(last_block, g * SUBS + i)
                                if last_block and g * SUBS + i == WIDE_FROM:
                                    pe.wait_ge(s["mx"], (b + 1) * (UNITS * 16) + MX_RING)
                                pe.wait_ge(s["probs"], first + (i + 1 + S_RING - ring))
                                mm(bank[sbank][:], kaug[:, g, kc * P:(kc + 1) * P],
                                   qaug[:, G * g + h, bass.ds(qt * QB, QB)], start=True, stop=True).then_inc(s["s_ps"], 1)
                                if not (last_block and rel >= BU):
                                    for k in MAXIMA_AFTER[h]:
                                        maxima(mfirst, *unit_at(rel, qt), 4 * (kc % 4) + k)
                                wide = last_block and g * SUBS + G * kc >= WIDE_FROM
                                if h == (G - 1 if wide else AV_AFTER) and kc >= 1:
                                    if kc == 1:
                                        pe.wait_ge(s["osb1"], grp0 + (g + 1))
                                    weighted(first, g, kc - 1)
                            if kc == OUT_AT and (g > 0 or not first_block):
                                to_queries(grp0 + (g - 1))
                            if kc in TURN_AT and g == 0 and not first_block:
                                turn(blk - 1, TURN_AT.index(kc), base + (G + 1))
                            if kc in PROJ_AT and g == 0 and not first_block:
                                project(blk - 1, PROJ_AT.index(kc), base + (G + 2 if kc < 10 else G + 3))
                            rel = G * g + G + kc // 4
                            if kc in SHIFT_AT and not (last_block and rel >= BU):
                                if kc == 2:
                                    pe.wait_ge(s["on1"], grp0 + (g + 1))
                                if kc == 6 and g == 0 and not first_block:
                                    pe.wait_ge(s["turn"], blk * 2)
                                if kc == 10 and g == 0 and not first_block:
                                    pe.wait_ge(s["y"], blk * RB)
                                if kc == 14 and g == 0 and not first_block:
                                    pe.wait_ge(s["y"], blk * RB + 1)
                                shift_rows(base + rel, rel % 2)
                        weighted(first, g, KC - 1)

                pe.wait_ge(s["xres"], (b + 1) * TILES + W)
                pe.wait_ge(s["v1"], (b + 1) * TILES)
                for rel in range(LEAD):
                    first = pe.snap((b * UNITS + rel) * 16)
                    for k in range(16):
                        maxima(first, *unit_at(rel, 0), k)
                    if rel >= 1:
                        shift_rows(b * UNITS + (rel - 1), (rel - 1) % 2)
                block_pe(0, True, False)
                with pe.Fori(1, QT - 1) as qt:
                    block_pe(qt, False, False)
                block_pe(QT - 1, False, True)
                to_queries((b + 1) * (QT * KV) - 1)
                for half in range(2):
                    turn(b * QT + (QT - 1), half, (b + 1) * UNITS)
                for r in range(RB):
                    project(b * QT + (QT - 1), r, (b + 1) * UNITS)

    return nc


_INS = ["L0_attn_x", "L0_attn_W_qkv", "L0_attn_W_out", "L0_ffn_weight", "L0_ffn_alpha", "L0_ffn_bias",
        "L1_attn_Wq", "L1_attn_bq", "L1_attn_Wk", "L1_attn_bk", "L1_attn_Wv", "L1_attn_bv", "L1_attn_Wo", "L1_attn_bo",
        "L1_ffn_gate_w", "L1_ffn_Wu", "L1_ffn_Wv", "L1_ffn_Wo"]


def kernel(**inputs):
    import numpy as _np
    import concourse.bacc as _bacc
    from concourse import mybir as _mybir
    from concourse.bass_utils import run_bass_kernel_spmd as _run

    nc = _bacc.Bacc("TRN2", target_bir_lowering=False, num_devices=1)
    arrays, args = {}, []
    for name in _INS:
        a = _np.ascontiguousarray(inputs[name])
        arrays[f"in_{name}_dram"] = a
        args.append(nc.dram_tensor(f"in_{name}_dram", a.shape, _mybir.dt.from_np(a.dtype), kind="ExternalInput").ap())
    args.append(nc.dram_tensor("out_0_dram", (B, S, D), _mybir.dt.float32, kind="ExternalOutput").ap())
    two_layers(nc, *args)
    r = _run(nc, [arrays], core_ids=[0])
    return r.results[0]["out_0_dram"]
```
